# Optimizing a Trainium2 kernel written in Bass

```python
import numpy as np
import jax
import jax.numpy as jnp

def _softmax(x, axis=-1):
    return jax.nn.softmax(x, axis=axis)
def _gelu(x):
    return jax.nn.gelu(x, approximate=True)
def _silu(x):
    return jax.nn.silu(x)
def _sigmoid(x):
    return jax.nn.sigmoid(x)
def _layernorm(x, axis=-1, eps=1e-5):
    m = jnp.mean(x, axis=axis, keepdims=True)
    v = jnp.var(x, axis=axis, keepdims=True)
    return (x - m) / jnp.sqrt(v + eps)
def _scatter_add(tgt, idx, src, axis=0):
    return tgt.at[idx].add(src)
def _segment_sum(src, seg, n):
    return jax.ops.segment_sum(src, seg, n)

kernel_name = 'mk_conv_seq_d2_conv_nchw512_8b27bb'

def setup_inputs(seed: int = 0):
    np.random.seed(seed)
    _w = jnp.asarray
    def _rec_inputs():
        import jax
        import jax.numpy as jnp
        _gk = jax.random.key(seed)
        x = -0.0005207 + 1.001 * jax.random.normal(jax.random.fold_in(_gk, 1), (1, 512, 64, 64), jnp.float32)
        return x
    x = _rec_inputs()
    def _L0_conv_setup():
        import jax, jax.numpy as jnp
        import numpy as np
        DIM = 512
        NUM_GROUPS = 32
        HEADS = 16
        HEAD_DIM = 32
        EPS = 1e-06

        def group_norm(x, w, b, num_groups=NUM_GROUPS, eps=EPS):
            B, C, H, W = x.shape
            xg = x.reshape(B, num_groups, -1)
            mean = xg.mean(axis=-1, keepdims=True)
            var = xg.var(axis=-1, keepdims=True)
            xg = (xg - mean) / jnp.sqrt(var + eps)
            x = xg.reshape(B, C, H, W)
            return x * w[None, :, None, None] + b[None, :, None, None]

        def conv1x1(x, w, b):
            return jnp.einsum('bchw,oc->bohw', x, w) + b[None, :, None, None]
        key = jax.random.key(seed)
        ks = jax.random.split(key, 12)
        s = 1.0 / np.sqrt(DIM)
        d = {'x': jax.random.normal(ks[0], (1, DIM, 64, 64), dtype=jnp.float32), 'gn_w': jnp.ones((DIM,), dtype=jnp.float32), 'gn_b': jnp.zeros((DIM,), dtype=jnp.float32), 'wq': jax.random.normal(ks[1], (DIM, DIM), dtype=jnp.float32) * s, 'bq': jax.random.normal(ks[2], (DIM,), dtype=jnp.float32) * 0.01, 'wk': jax.random.normal(ks[3], (DIM, DIM), dtype=jnp.float32) * s, 'bk': jax.random.normal(ks[4], (DIM,), dtype=jnp.float32) * 0.01, 'wv': jax.random.normal(ks[5], (DIM, DIM), dtype=jnp.float32) * s, 'bv': jax.random.normal(ks[6], (DIM,), dtype=jnp.float32) * 0.01, 'wo': jax.random.normal(ks[7], (DIM, DIM), dtype=jnp.float32) * s, 'bo': jax.random.normal(ks[8], (DIM,), dtype=jnp.float32) * 0.01}
        return d
    _L0_conv_all = _L0_conv_setup()
    _L0_conv_in = {k: v for k, v in _L0_conv_all.items() if k in ('gn_w', 'gn_b', 'wq', 'bq', 'wk', 'bk', 'wv', 'bv', 'wo', 'bo', )}
    del _L0_conv_all

    def _L1_conv_setup():
        import jax, jax.numpy as jnp
        import numpy as np
        DIM = 8
        HEADS = 64
        INNER = HEADS * DIM
        CIN = 512
        COUT = 512
        SCALE = 5
        G = 3 * HEADS
        EPS_ATT = 1e-15
        EPS_BN = 1e-05

        def _aggreg(qkv, w_dw, w_pw):
            y = jax.lax.conv_general_dilated(qkv, w_dw, window_strides=(1, 1), padding=[(2, 2), (2, 2)], dimension_numbers=('NCHW', 'OIHW', 'NCHW'), feature_group_count=3 * INNER)
            B, C, H, W = y.shape
            yg = y.reshape(B, G, DIM, H, W)
            out = jnp.einsum('gok,bgkhw->bgohw', w_pw, yg)
            return out.reshape(B, C, H, W)

        def _relu_linear_att(qkv):
            B, C, H, W = qkv.shape
            N = H * W
            qkv = qkv.astype(jnp.float32).reshape(B, -1, 3 * DIM, N)
            q = jax.nn.relu(qkv[:, :, :DIM])
            k = jax.nn.relu(qkv[:, :, DIM:2 * DIM])
            v = qkv[:, :, 2 * DIM:]
            v1 = jnp.concatenate([v, jnp.ones_like(v[:, :, :1])], axis=2)
            vk = jnp.einsum('bhdn,bhen->bhde', v1, k)
            out = jnp.einsum('bhde,bhen->bhdn', vk, q)
            out = out[:, :, :-1] / (out[:, :, -1:] + EPS_ATT)
            return out.reshape(B, -1, H, W)
        key = jax.random.key(seed)
        ks = jax.random.split(key, 7)
        B, H, W = (2, 128, 128)
        x = jax.random.normal(ks[0], (B, CIN, H, W), dtype=jnp.float32)
        w_qkv = jax.random.normal(ks[1], (3 * INNER, CIN), dtype=jnp.float32) * 0.02
        w_dw = jax.random.normal(ks[2], (3 * INNER, 1, SCALE, SCALE), dtype=jnp.float32) * 0.05
        w_pw = jax.random.normal(ks[3], (G, DIM, DIM), dtype=jnp.float32) * 0.1
        w_proj = jax.random.normal(ks[4], (COUT, 2 * INNER), dtype=jnp.float32) * 0.02
        bn_gamma = jnp.ones((COUT,), dtype=jnp.float32)
        bn_beta = jnp.zeros((COUT,), dtype=jnp.float32)
        return {'x': x, 'w_qkv': w_qkv, 'w_dw': w_dw, 'w_pw': w_pw, 'w_proj': w_proj, 'bn_gamma': bn_gamma, 'bn_beta': bn_beta}
    _L1_conv_all = _L1_conv_setup()
    _L1_conv_in = {k: v for k, v in _L1_conv_all.items() if k in ('w_qkv', 'w_dw', 'w_pw', 'w_proj', 'bn_gamma', 'bn_beta', )}
    del _L1_conv_all

    return {
        "x": x,
        "L0_conv_gn_w": _L0_conv_in["gn_w"],
        "L0_conv_gn_b": _L0_conv_in["gn_b"],
        "L0_conv_wq": _L0_conv_in["wq"],
        "L0_conv_bq": _L0_conv_in["bq"],
        "L0_conv_wk": _L0_conv_in["wk"],
        "L0_conv_bk": _L0_conv_in["bk"],
        "L0_conv_wv": _L0_conv_in["wv"],
        "L0_conv_bv": _L0_conv_in["bv"],
        "L0_conv_wo": _L0_conv_in["wo"],
        "L0_conv_bo": _L0_conv_in["bo"],
        "L1_conv_w_qkv": _L1_conv_in["w_qkv"],
        "L1_conv_w_dw": _L1_conv_in["w_dw"],
        "L1_conv_w_pw": _L1_conv_in["w_pw"],
        "L1_conv_w_proj": _L1_conv_in["w_proj"],
        "L1_conv_bn_gamma": _L1_conv_in["bn_gamma"],
        "L1_conv_bn_beta": _L1_conv_in["bn_beta"],
    }

def reference(x, L0_conv_gn_w, L0_conv_gn_b, L0_conv_wq, L0_conv_bq, L0_conv_wk, L0_conv_bk, L0_conv_wv, L0_conv_bv, L0_conv_wo, L0_conv_bo, L1_conv_w_qkv, L1_conv_w_dw, L1_conv_w_pw, L1_conv_w_proj, L1_conv_bn_gamma, L1_conv_bn_beta):
    import jax
    import jax.numpy as jnp
    def _L0_conv_ref(x, gn_w, gn_b, wq, bq, wk, bk, wv, bv, wo, bo):
        import jax, jax.numpy as jnp
        import numpy as np
        DIM = 512
        NUM_GROUPS = 32
        HEADS = 16
        HEAD_DIM = 32
        EPS = 1e-06

        def group_norm(x, w, b, num_groups=NUM_GROUPS, eps=EPS):
            B, C, H, W = x.shape
            xg = x.reshape(B, num_groups, -1)
            mean = xg.mean(axis=-1, keepdims=True)
            var = xg.var(axis=-1, keepdims=True)
            xg = (xg - mean) / jnp.sqrt(var + eps)
            x = xg.reshape(B, C, H, W)
            return x * w[None, :, None, None] + b[None, :, None, None]

        def conv1x1(x, w, b):
            return jnp.einsum('bchw,oc->bohw', x, w) + b[None, :, None, None]
        B, C, H, W = x.shape
        N = H * W
        scale = HEAD_DIM ** (-0.5)
        q_in = x
        qn = group_norm(x, gn_w, gn_b)
        vn = group_norm(qn, gn_w, gn_b)
        q = conv1x1(qn, wq, bq)
        k = conv1x1(vn, wk, bk)
        v = conv1x1(vn, wv, bv)

        def to_tokens(t):
            return t.reshape(B, HEADS, HEAD_DIM, N).transpose(0, 1, 3, 2)
        q, k, v = (to_tokens(q), to_tokens(k), to_tokens(v))
        attn = jax.nn.softmax(jnp.einsum('bhnd,bhmd->bhnm', q, k) * scale, axis=-1)
        out = jnp.einsum('bhnm,bhmd->bhnd', attn, v)
        out = out.transpose(0, 1, 3, 2).reshape(B, C, H, W)
        out = conv1x1(out, wo, bo)
        return (out + q_in) / jnp.sqrt(jnp.float32(2.0))

    def _L1_conv_ref(x, w_qkv, w_dw, w_pw, w_proj, bn_gamma, bn_beta):
        import jax, jax.numpy as jnp
        import numpy as np
        DIM = 8
        HEADS = 64
        INNER = HEADS * DIM
        CIN = 512
        COUT = 512
        SCALE = 5
        G = 3 * HEADS
        EPS_ATT = 1e-15
        EPS_BN = 1e-05

        def _aggreg(qkv, w_dw, w_pw):
            y = jax.lax.conv_general_dilated(qkv, w_dw, window_strides=(1, 1), padding=[(2, 2), (2, 2)], dimension_numbers=('NCHW', 'OIHW', 'NCHW'), feature_group_count=3 * INNER)
            B, C, H, W = y.shape
            yg = y.reshape(B, G, DIM, H, W)
            out = jnp.einsum('gok,bgkhw->bgohw', w_pw, yg)
            return out.reshape(B, C, H, W)

        def _relu_linear_att(qkv):
            B, C, H, W = qkv.shape
            N = H * W
            qkv = qkv.astype(jnp.float32).reshape(B, -1, 3 * DIM, N)
            q = jax.nn.relu(qkv[:, :, :DIM])
            k = jax.nn.relu(qkv[:, :, DIM:2 * DIM])
            v = qkv[:, :, 2 * DIM:]
            v1 = jnp.concatenate([v, jnp.ones_like(v[:, :, :1])], axis=2)
            vk = jnp.einsum('bhdn,bhen->bhde', v1, k)
            out = jnp.einsum('bhde,bhen->bhdn', vk, q)
            out = out[:, :, :-1] / (out[:, :, -1:] + EPS_ATT)
            return out.reshape(B, -1, H, W)
        residual = x
        qkv = jnp.einsum('oc,bchw->bohw', w_qkv, x)
        qkv_ms = jnp.concatenate([qkv, _aggreg(qkv, w_dw, w_pw)], axis=1)
        out = _relu_linear_att(qkv_ms).astype(qkv_ms.dtype)
        out = jnp.einsum('oc,bchw->bohw', w_proj, out)
        mean = jnp.mean(out, axis=(0, 2, 3), keepdims=True)
        var = jnp.var(out, axis=(0, 2, 3), keepdims=True)
        out = (out - mean) * jax.lax.rsqrt(var + EPS_BN)
        out = out * bn_gamma[None, :, None, None] + bn_beta[None, :, None, None]
        return out + residual

    def _gn(v, G=32, eps=1e-5):
        B_, C_, H_, W_ = v.shape
        g = v.reshape(B_, G, C_ // G, H_, W_)
        m = jnp.mean(g, axis=(2, 3, 4), keepdims=True)
        s = jnp.var(g, axis=(2, 3, 4), keepdims=True)
        return ((g - m) / jnp.sqrt(s + eps)).reshape(v.shape)

    def _ln_c(v, eps=1e-6):
        m = jnp.mean(v, axis=1, keepdims=True)
        s = jnp.var(v, axis=1, keepdims=True)
        return (v - m) / jnp.sqrt(s + eps)

    def _ln_t(v, eps=1e-5):
        m = jnp.mean(v, axis=-1, keepdims=True)
        s = jnp.var(v, axis=-1, keepdims=True)
        return (v - m) / jnp.sqrt(s + eps)

    def _to_tokens(v):
        B_, C_, H_, W_ = v.shape
        return v.reshape(B_, C_, H_ * W_).transpose(0, 2, 1)
    def _from_tokens(t, like):
        B_, C_, H_, W_ = like.shape
        return t.transpose(0, 2, 1).reshape(B_, C_, H_, W_)

    x = _L0_conv_ref(x, L0_conv_gn_w, L0_conv_gn_b, L0_conv_wq, L0_conv_bq, L0_conv_wk, L0_conv_bk, L0_conv_wv, L0_conv_bv, L0_conv_wo, L0_conv_bo)
    x = _L1_conv_ref(x, L1_conv_w_qkv, L1_conv_w_dw, L1_conv_w_pw, L1_conv_w_proj, L1_conv_bn_gamma, L1_conv_bn_beta)
    return x


_drawn_inputs = setup_inputs


def setup_inputs(seed=0):
    import zlib

    import numpy as np

    out = dict(_drawn_inputs(seed))
    spreads = {'L0_conv_gn_w': (1.0, 0.2),
     'L0_conv_gn_b': (0.0, 0.1),
     'L1_conv_bn_gamma': (1.0, 0.2),
     'L1_conv_bn_beta': (0.0, 0.1)}
    factors = {}
    for name, (base, spread) in spreads.items():
        noise = np.random.default_rng([zlib.crc32(name.encode()), seed]).standard_normal(out[name].shape)
        drawn = base * np.exp(spread * noise) if base else spread * noise
        out[name] = jnp.asarray(drawn.astype(out[name].dtype))
    for name, factor in factors.items():
        out[name] = (out[name] * factor).astype(out[name].dtype)
    return out
```

```python
from contextlib import ExitStack

import concourse.bass as bass
from concourse import mybir

F32 = mybir.dt.float32
F32R = mybir.dt.float32r
ALU = mybir.AluOpType
ACT = mybir.ActivationFunctionType
AX = mybir.AxisListType

P = 128
C = 512
IMG = 64
N = IMG * IMG
KC = C // P
BANK = 512
CHUNKS = N // BANK

GN_GROUP = 16
GN_EPS = 1e-6
HEADS = 16
HD = C // HEADS
SCALE = float(HD) ** -0.5

CREDIT = 8


def done(n):
    return n + CREDIT


class Scratch:

    def __init__(self, nc):
        self.qh = nc.dram_tensor("scratch_qh", (C, N), F32, kind="Internal").ap()
        self.ql = nc.dram_tensor("scratch_ql", (C, N), F32, kind="Internal").ap()
        self.kh = nc.dram_tensor("scratch_kh", (C, N), F32, kind="Internal").ap()
        self.kl = nc.dram_tensor("scratch_kl", (C, N), F32, kind="Internal").ap()
        self.num = nc.dram_tensor("scratch_num", (2, GROUPS, P, N), F32, kind="Internal").ap()
        self.den = nc.dram_tensor("scratch_den", (2, GROUPS, HPG, N), F32, kind="Internal").ap()
        self.rden = nc.dram_tensor("scratch_rden", (2 * GROUPS * HPG, N), F32, kind="Internal").ap()
        self.att = nc.dram_tensor("scratch_att", (C, N), F32, kind="Internal").ap()


def stage_qkv(nc, x, chan, wqT, wkT, wvT, bv, group_mean, scr, v_tok):
    with ExitStack() as ctx:
        def sb(name, shape, dt=F32):
            return ctx.enter_context(nc.sbuf_tensor(name, shape, dt))

        def sem(name):
            return ctx.enter_context(nc.semaphore(name))

        xs = sb("a_x", [P, KC, N])
        w = {r: sb(f"a_w{r}", [P, KC, C]) for r in "qkv"}
        par = sb("a_par", [P, KC, 4])
        bv_rows = sb("a_bv_rows", [P, C])
        gmean = sb("a_gmean", [P, P])
        stats = sb("a_stats", [P, KC, CHUNKS, 6])
        mv = sb("a_mv", [P, KC, 2])
        dev = sb("a_dev", [P, KC])
        spread = sb("a_spread", [P, KC])
        mean = sb("a_mean", [P, KC])
        rstd = sb("a_rstd", [P, KC])
        tmp = sb("a_tmp", [P, KC])
        var = sb("a_var", [P, KC])
        sd = sb("a_sd", [P, KC])
        aff = sb("a_aff", [P, 2, 2, KC])
        vn = sb("a_vn", [P, 2, KC, BANK])
        high = sb("a_high", [P, 2, 4, BANK], F32R)
        low = sb("a_low", [P, 2, 4, BANK], F32R)
        ps = [ctx.enter_context(nc.psum_tensor(f"a_ps{i}", [P, BANK], F32)) for i in range(8)]

        x_in = sem("a_x_in")
        par_in = sem("a_par_in")
        w_in = sem("a_w_in")
        stat = sem("a_stat")
        moments = sem("a_moments")
        spread_ready = sem("a_spread_ready")
        gsum = sem("a_gsum")
        var_ready = sem("a_var_ready")
        root = sem("a_root")
        coef = sem("a_coef")
        qn_ready = sem("a_qn_ready")
        vn_ready = sem("a_vn_ready")
        mm_done = sem("a_mm_done")
        high_done = sem("a_high_done")
        low_done = sem("a_low_done")
        v_done = sem("a_v_done")
        stored = [sem(f"a_stored_{r}") for r in "qk"]

        TILES = 12
        block = ctx.enter_context(nc.Block())

        @block.sync
        def _(sp):
            for k in range(KC):
                sp.dma_start(xs[:, k, :], x[k * P:(k + 1) * P, :]).then_inc(x_in, 16)
            sp.dma_start(par[:], chan).then_inc(par_in, 16)
            sp.dma_start(gmean[:], group_mean).then_inc(par_in, 16)
            sp.dma_start(bv_rows[:], bv.partition_broadcast(P)).then_inc(par_in, 16)
            for r, src in (("q", wqT), ("k", wkT), ("v", wvT)):
                sp.dma_start(w[r][:], src.rearrange("(k p) o -> p k o", p=P)).then_inc(w_in, 16)
            with sp.Fori(0, CHUNKS // 2) as i:
                for b in range(2):
                    n = i * 2 + b
                    for r, (hi_d, lo_d) in enumerate(((scr.qh, scr.ql), (scr.kh, scr.kl))):
                        sp.wait_ge(low_done, done(n * 8 + 4 * r + 4))
                        for dst, src in ((hi_d, high), (lo_d, low)):
                            sp.dma_start(
                                dst.rearrange("(k p) n -> p k n", p=P)[:, :, bass.ds(n * BANK, BANK)],
                                src[:, r, :, :].bitcast(F32)).then_inc(stored[r], 16)
            for s in stored:
                sp.wait_ge(s, done(CHUNKS * 2 * 16))

        @block.vector
        def _(dve):
            for s in (low_done, v_done):
                dve.sem_inc(s, CREDIT)
            links = 0

            def link(ins):
                nonlocal links
                links += 1
                ins.then_inc(stat, 1)
                dve.wait_ge(stat, links)

            for k in range(KC):
                dve.wait_ge(x_in, 16 * KC)
                for j in range(CHUNKS):
                    last = dve.bn_stats(stats[:, k, j, :], xs[:, k, j * BANK:(j + 1) * BANK])
            link(last)
            for k in range(KC):
                last = dve.bn_aggr(mv[:, k, :], stats[:, k, :, :].rearrange("p j s -> p (j s)"))
            link(last)
            dve.wait_ge(par_in, 16 * 3)

            def affine(norm):
                dve.sem_inc(moments, 1)
                dve.wait_ge(gsum, 2 * norm + 1)
                link(dve.tensor_copy(mean[:], ps[0][:, 0:KC]))
                link(dve.tensor_tensor(dev[:], mv[:, :, 0], mean[:], ALU.subtract))
                link(dve.tensor_tensor(dev[:], dev[:], dev[:], ALU.mult))
                dve.tensor_tensor(spread[:], dev[:], mv[:, :, 1], ALU.add).then_inc(spread_ready, 1)
                dve.wait_ge(gsum, 2 * norm + 2)
                dve.tensor_scalar(var[:], ps[1][:, 0:KC], GN_EPS, None, ALU.add).then_inc(var_ready, 1)
                dve.wait_ge(root, norm + 1)
                link(dve.reciprocal(rstd[:], sd[:]))
                link(dve.tensor_tensor(tmp[:], rstd[:], rstd[:], ALU.mult))
                link(dve.tensor_tensor(tmp[:], tmp[:], var[:], ALU.mult))
                link(dve.tensor_scalar(tmp[:], tmp[:], -0.5, 1.5, ALU.mult, ALU.add))
                link(dve.tensor_tensor(rstd[:], rstd[:], tmp[:], ALU.mult))
                link(dve.tensor_tensor(aff[:, norm, 0, :], rstd[:], par[:, :, 0], ALU.mult))
                link(dve.tensor_tensor(tmp[:], mean[:], aff[:, norm, 0, :], ALU.mult))
                return dve.tensor_tensor(aff[:, norm, 1, :], par[:, :, 1], tmp[:], ALU.subtract)

            link(affine(0))
            link(dve.tensor_tensor(tmp[:], mv[:, :, 0], aff[:, 0, 0, :], ALU.mult))
            link(dve.tensor_tensor(mv[:, :, 0], tmp[:], aff[:, 0, 1, :], ALU.add))
            link(dve.tensor_tensor(tmp[:], mv[:, :, 1], aff[:, 0, 0, :], ALU.mult))
            link(dve.tensor_tensor(mv[:, :, 1], tmp[:], aff[:, 0, 0, :], ALU.mult))
            link(affine(1))
            dve.sem_inc(coef, 1)
            for k in range(KC):
                dve.tensor_scalar(xs[:, k, :], xs[:, k, :], aff[:, 0, 0, k:k + 1],
                                  aff[:, 0, 1, k:k + 1], ALU.mult, ALU.add).then_inc(qn_ready, 1)

            with dve.Fori(0, CHUNKS // 2) as i:
                for b in range(2):
                    n = i * 2 + b
                    for m in range(8):
                        r, t = m // 4, m % 4
                        g = b * TILES + m
                        dve.wait_ge(high_done, done(n * 8 + m + 1))
                        if t == 0:
                            dve.wait_ge(stored[r], done(n * 32))
                        bias = par[:, t, 2 + r:3 + r]
                        dve.scalar_tensor_tensor(low[:, r, t, :], ps[g % 8][:], bias,
                                                 high[:, r, t, :].bitcast(F32), ALU.add,
                                                 ALU.subtract).then_inc(low_done, 1)
                    for t in range(4):
                        g = b * TILES + 8 + t
                        dve.wait_ge(mm_done, done(n * TILES + 8 + t + 1))
                        dve.tensor_tensor(v_tok[:, n * 4 + t, :], ps[g % 8][:], bv_rows[:],
                                          ALU.add).then_inc(v_done, 1)

        @block.scalar
        def _(act):
            act.sem_inc(high_done, CREDIT)
            act.sem_inc(vn_ready, CREDIT)
            for norm in range(2):
                act.wait_ge(var_ready, norm + 1)
                act.activation(sd[:], var[:], ACT.Sqrt).then_inc(root, 1)
            act.wait_ge(coef, 1)
            act.wait_ge(qn_ready, KC)

            def normalise(n, b):
                for k in range(KC):
                    last = act.activation(vn[:, b, k, :], xs[:, k, bass.ds(n * BANK, BANK)], ACT.Identity,
                                          bias=aff[:, 1, 1, k:k + 1], scale=aff[:, 1, 0, k:k + 1])
                last.then_inc(vn_ready, 1)

            def pair(i, final):
                for b in range(2):
                    n = i * 2 + b
                    if not (final and b == 1):
                        act.wait_ge(mm_done, done(n * TILES))
                        normalise(n + 1, 1 - b)
                    for m in range(8):
                        r, t = m // 4, m % 4
                        g = b * TILES + m
                        act.wait_ge(mm_done, done(n * TILES + m + 1))
                        if t == 0:
                            act.wait_ge(stored[r], done(n * 32))
                            act.wait_ge(low_done, done(n * 8))
                        act.activation(high[:, r, t, :], ps[g % 8][:], ACT.Identity,
                                       bias=par[:, t, 2 + r:3 + r]).then_inc(high_done, 1)

            normalise(0, 0)
            with act.Fori(0, CHUNKS // 2 - 1) as i:
                pair(i, False)
            pair(CHUNKS // 2 - 1, True)

        @block.tensor
        def _(pe):
            for s in (mm_done, *stored):
                pe.sem_inc(s, CREDIT)
            pe.wait_ge(par_in, 16 * 3)
            for norm in range(2):
                pe.wait_ge(moments, norm + 1)
                pe.matmul(ps[0][:, 0:KC], gmean[:], mv[:, :, 0], start=True, stop=True).then_inc(gsum, 1)
                pe.wait_ge(spread_ready, norm + 1)
                pe.matmul(ps[1][:, 0:KC], gmean[:], spread[:], start=True, stop=True).then_inc(gsum, 1)
            pe.wait_ge(qn_ready, KC)
            pe.wait_ge(w_in, 16 * 3)
            with pe.Fori(0, CHUNKS // 2) as i:
                for b in range(2):
                    n = i * 2 + b
                    for m in range(TILES):
                        g = b * TILES + m
                        if m == 0:
                            pe.wait_ge(v_done, done(n * 4))
                        if m == 4:
                            pe.wait_ge(vn_ready, done(n + 1))
                        if m < 4:
                            pe.wait_ge(low_done, done(n * 8))
                        elif m >= 8:
                            pe.wait_ge(low_done, done(n * 8 + m - 8 + 1))
                        r, t = m // 4, m % 4
                        for k in range(KC):
                            if r == 0:
                                lhs, rhs = w["q"][:, k, t * P:(t + 1) * P], xs[:, k, bass.ds(n * BANK, BANK)]
                            elif r == 1:
                                lhs, rhs = w["k"][:, k, t * P:(t + 1) * P], vn[:, b, k, :]
                            else:
                                lhs, rhs = vn[:, b, k, t * P:(t + 1) * P], w["v"][:, k, :]
                            last = pe.matmul(ps[g % 8][:], lhs, rhs, start=(k == 0), stop=(k == KC - 1))
                        last.then_inc(mm_done, 1)


def stage_attention(nc, scr, v_tok, ident_d):
    UNIT = 1024
    UNITS = N // UNIT
    KT = N // P
    ROWS = 3 * HD
    SHIFT_AT = ROWS
    FULL = ROWS + 2
    QT = UNIT // P
    MAXES = QT * CHUNKS
    SLOTS = MAXES + 1
    PAIR = 2
    PBUF = 4
    with ExitStack() as ctx:
        def sb(name, shape, dt=F32):
            return ctx.enter_context(nc.sbuf_tensor(name, shape, dt))

        def pb(name, shape):
            return ctx.enter_context(nc.psum_tensor(name, shape, F32))

        def sem(name):
            return ctx.enter_context(nc.semaphore(name))

        kst = sb("b_kst", [P, 2, N], F32R)
        qst = sb("b_qst", [P, 2, UNIT], F32R)
        vst = sb("b_vst", [P, 2, KT, 2 * HD])
        prob = sb("b_prob", [P, PBUF, UNIT])
        mx = sb("b_mx", [P, QT, CHUNKS])
        mtop = sb("b_mtop", [P, QT])
        mneg = sb("b_mneg", [P, 2 * QT])
        mrow = sb("b_mrow", [2 * QT, P], F32R)
        rden = sb("b_rden", [P, BANK])
        outn = sb("b_outn", [P, 2, BANK])
        ident = sb("b_ident", [P, P])
        pscore = [pb(f"b_pscore{i}", [P, UNIT]) for i in range(2)]
        pmax = [pb(f"b_pmax{i}", [P, BANK]) for i in range(2)]
        pout = [pb(f"b_pout{i}", [P, BANK]) for i in range(2)]

        consts = sem("b_consts")
        k_in = [sem(f"b_k_in{i}") for i in range(2)]
        q_in = [sem(f"b_q_in{i}") for i in range(2)]
        v_in = sem("b_v_in")
        shift_in = sem("b_shift_in")
        scored = sem("b_scored")
        exped = sem("b_exped")
        summed = sem("b_summed")
        max_mm = sem("b_max_mm")
        max_read = sem("b_max_read")
        mlink = sem("b_mlink")
        packed = sem("b_packed")
        nlink = sem("b_nlink")
        out_ready = sem("b_out_ready")
        stored = [sem(f"b_stored{i}") for i in range(2)]
        all_sems = (k_in[0], k_in[1], q_in[0], q_in[1], v_in, shift_in, scored, exped,
                    summed, max_mm, max_read, mlink, nlink, packed, out_ready, *stored)

        heads = {n: a.rearrange("(h d) n -> h d n", d=HD) for n, a in
                 (("qh", scr.qh), ("ql", scr.ql), ("kh", scr.kh), ("kl", scr.kl), ("att", scr.att))}
        block = ctx.enter_context(nc.Block())

        def units(i):
            for par in range(PAIR):
                for c in range(UNITS):
                    yield (i * PAIR + par) * UNITS + c, i * PAIR + par, par, c

        TURNS = HEADS // PAIR

        @block.sync
        def _(sp):
            for s in all_sems:
                sp.sem_inc(s, CREDIT)
            sp.dma_start(ident[:], ident_d).then_inc(consts, 16)

            def load_k(head, par):
                for row, name in ((0, "kh"), (HD, "kl"), (2 * HD, "kh")):
                    sp.dma_start(kst[row:row + HD, par, :].bitcast(F32), heads[name][head]).then_inc(k_in[par], 16)

            def load_q(head, c, b):
                for row, name in ((0, "qh"), (HD, "qh"), (2 * HD, "ql")):
                    sp.dma_start(qst[row:row + HD, b, :].bitcast(F32),
                                 heads[name][head, :, c * UNIT:(c + 1) * UNIT]).then_inc(q_in[b], 16)

            def load_shift(u, b):
                sp.wait_ge(max_read, done((u + 1) * SLOTS))
                for half in range(2):
                    sp.dma_start(qst[SHIFT_AT + half:SHIFT_AT + half + 1, b, :].bitcast(F32).rearrange(
                        "o (t j) -> o t j", j=P), mrow[half * QT:(half + 1) * QT, :].bitcast(F32)).then_inc(shift_in, 16)

            def store(u, head, c):
                sp.wait_ge(out_ready, done(u + 1))
                for half in (1, 0):
                    at = c * UNIT + half * BANK
                    sp.dma_start(heads["att"][head, :, at:at + BANK],
                                 outn[2 * HD * half:2 * HD * half + HD, c % 2, :]).then_inc(stored[c % 2], 16)

            load_k(0, 0)
            load_q(0, 0, 0)
            load_q(0, 1, 1)
            load_k(1, 1)
            load_shift(0, 0)

            def turn(i, final):
                for u, head, par, c in units(i):
                    if not (par == 0 and c == 0):
                        store(u - 1, head if c else head - 1, (c - 1) % UNITS)
                    last = final and par == PAIR - 1 and c == UNITS - 1
                    if not last:
                        load_shift(u + 1, (c + 1) % 2)
                    sp.wait_ge(scored, done((u + 1) * KT))
                    nxt = par * UNITS + c + 2
                    if not (final and nxt >= PAIR * UNITS):
                        load_q(i * PAIR + nxt // UNITS, nxt % UNITS, c % 2)
                    if c == UNITS - 1 and not final:
                        load_k(head + PAIR, par)
                store((i + 1) * PAIR * UNITS - 1, i * PAIR + PAIR - 1, UNITS - 1)

            with sp.Fori(0, TURNS - 1) as i:
                turn(i, False)
            turn(TURNS - 1, True)
            for s in stored:
                sp.wait_ge(s, done(HEADS * UNITS // 2 * 32))

        @block.gpsimd
        def _(pool):
            def copy_v(head, par):
                pool.tensor_copy(vst[:, par, :, 0:HD], v_tok[:, :, bass.ds(head * HD, HD)]).then_inc(v_in, 1)

            copy_v(0, 0)
            copy_v(1, 1)
            with pool.Fori(0, TURNS - 1) as i:
                for par in range(PAIR):
                    pool.wait_ge(summed, done((i * PAIR + par + 1) * UNITS * KT))
                    copy_v(i * PAIR + par + PAIR, par)

        def max_slots(kt):
            steps = KT - 4
            return [m for m in range(MAXES) if m * steps // MAXES == kt]

        @block.tensor
        def _(pe):
            pe.wait_ge(consts, 16 + 4)

            def max_product(u, m, par, b):
                t, j = m // CHUNKS, m % CHUNKS
                if m < 2:
                    pe.wait_ge(max_read, done(u * SLOTS))
                else:
                    pe.wait_ge(max_read, done(u * SLOTS + m - 1))
                pe.matmul(pmax[m % 2][:], qst[0:ROWS, b, t * P:(t + 1) * P],
                          kst[0:ROWS, par, j * BANK:(j + 1) * BANK], start=True,
                          stop=True).then_inc(max_mm, 1)

            def transpose_shift(u):
                pe.wait_ge(packed, done(u + 1))
                pe.wait_ge(max_read, done(u * SLOTS + MAXES - 1))
                pe.transpose(pmax[0][0:2 * QT, 0:P], mneg[:], ident[:]).then_inc(max_mm, 1)

            def times_v(u, par, c, kt):
                pe.wait_ge(exped, done(u * KT + kt + 1))
                for half in range(2):
                    last = pe.matmul(pout[c % 2][2 * HD * half:2 * HD * (half + 1), :], vst[:, par, kt, :],
                                     prob[:, kt % PBUF, half * BANK:(half + 1) * BANK],
                                     start=(kt == 0), stop=(kt == KT - 1))
                last.then_inc(summed, 1)

            pe.wait_ge(q_in[0], done(48))
            pe.wait_ge(k_in[0], done(48))
            for m in range(MAXES):
                max_product(0, m, 0, 0)
            transpose_shift(0)

            def turn(i, final):
                for u, head, par, c in units(i):
                    nu, npar, nc_ = u + 1, (par if c < UNITS - 1 else 1 - par), (c + 1) % UNITS
                    last = final and par == PAIR - 1 and c == UNITS - 1
                    if not last:
                        at = par * UNITS + c + 1
                        pe.wait_ge(q_in[(c + 1) % 2], done((i * (PAIR * UNITS // 2) + at // 2 + 1) * 48))
                        if nc_ == 0:
                            pe.wait_ge(k_in[npar], done((i + (1 if npar == 0 else 0) + 1) * 48))
                    pe.wait_ge(shift_in, done((u + 1) * 32))
                    for kt in range(KT):
                        pe.wait_ge(exped, done(u * KT + kt - 1))
                        for half in range(2):
                            at = slice(half * BANK, (half + 1) * BANK)
                            mm = pe.matmul(pscore[kt % 2][:, at], kst[0:FULL, par, kt * P:(kt + 1) * P],
                                           qst[0:FULL, c % 2, at], start=True, stop=True)
                        mm.then_inc(scored, 1)
                        if not last:
                            for m in max_slots(kt):
                                max_product(nu, m, npar, nc_ % 2)
                        if kt == KT - 3 and not last:
                            transpose_shift(nu)
                        if kt == 0 and not (par == c == 0):
                            times_v(u - 1, par if c else 1 - par, (c - 1) % UNITS, KT - 1)
                        if kt == 1:
                            if c == 0:
                                pe.wait_ge(v_in, done(head + 1))
                            pe.wait_ge(out_ready, done(u - 1))
                        if kt > 0:
                            times_v(u, par, c, kt - 1)
                times_v((i + 1) * PAIR * UNITS - 1, PAIR - 1, UNITS - 1, KT - 1)

            with pe.Fori(0, TURNS - 1) as i:
                turn(i, False)
            turn(TURNS - 1, True)

        @block.scalar
        def _(act):
            def turn(i):
                for u, head, par, c in units(i):
                    for kt in range(KT):
                        act.wait_ge(scored, done(u * KT + kt + 1))
                        act.wait_ge(summed, done(u * KT + kt + 1 - PBUF))
                        act.activation(prob[:, kt % PBUF, :], pscore[kt % 2][:], ACT.Exp,
                                       scale=SCALE).then_inc(exped, 1)

            with act.Fori(0, TURNS) as i:
                turn(i)

        @block.vector
        def _(dve):
            def small(u, n):
                dve.wait_ge(mlink, done(u * 2 + n))

            def read_max(u, m):
                t, j = m // CHUNKS, m % CHUNKS
                dve.wait_ge(max_mm, done(u * SLOTS + m + 1))
                return dve.tensor_reduce(mx[:, t, j:j + 1], pmax[m % 2][:], AX.X, ALU.max).then_inc(max_read, 1)

            def pack_shift(u):
                dve.wait_ge(max_read, done(u * SLOTS + MAXES))
                dve.tensor_reduce(mtop[:], mx[:], AX.X, ALU.max).then_inc(mlink, 1)
                small(u, 1)
                dve.wait_ge(max_mm, done(u * SLOTS))
                dve.tensor_scalar(mneg[:, 0:QT].bitcast(F32R), mtop[:], -1.0, None, ALU.mult).then_inc(mlink, 1)
                small(u, 2)
                dve.scalar_tensor_tensor(mneg[:, QT:2 * QT], mtop[:], -1.0, mneg[:, 0:QT], ALU.mult,
                                         ALU.subtract).then_inc(packed, 1)
                dve.wait_ge(max_mm, done(u * SLOTS + SLOTS))
                dve.wait_ge(shift_in, done(u * 32))
                dve.tensor_copy(mrow[:], pmax[0][0:2 * QT, 0:P]).then_inc(max_read, 1)

            def normalise(u, turns, b):
                dve.wait_ge(summed, done((u + 1) * KT))
                dve.wait_ge(out_ready, done(u))
                for half in range(2):
                    at = 2 * HD * half
                    dve.reciprocal(rden[at:at + HD, :], pout[b][at + HD:at + 2 * HD, :]).then_inc(nlink, 1)
                dve.wait_ge(stored[b], done(turns * 32))
                for half in range(2):
                    at = 2 * HD * half
                    dve.wait_ge(nlink, done(u * 2 + half + 1))
                    last = dve.tensor_tensor(outn[at:at + HD, b, :], pout[b][at:at + HD, :],
                                             rden[at:at + HD, :], ALU.mult)
                last.then_inc(out_ready, 1)

            for par in range(2):
                dve.memset(kst[ROWS:P, par, :].bitcast(F32), 1.0).then_inc(consts, 1)
                dve.memset(vst[:, par, :, HD:], 1.0).then_inc(consts, 1)
            for m in range(MAXES):
                read_max(0, m)
            pack_shift(0)

            def turn(i, final):
                for u, head, par, c in units(i):
                    last = final and par == PAIR - 1 and c == UNITS - 1
                    for m in range(MAXES):
                        if not last:
                            read_max(u + 1, m)
                        if m == 4 and not (par == c == 0):
                            normalise(u - 1, i * (PAIR * UNITS // 2) + (par * UNITS + c - 1) // 2, (c - 1) % 2)
                    if not last:
                        pack_shift(u + 1)
                normalise((i + 1) * PAIR * UNITS - 1, (i + 1) * (PAIR * UNITS // 2) - 1, 1)

            with dve.Fori(0, TURNS - 1) as i:
                turn(i, False)
            turn(TURNS - 1, True)


def stage_output(nc, x, chan_o, woT, scr, x1):
    R2 = 0.5 ** 0.5
    with ExitStack() as ctx:
        def sb(name, shape, dt=F32):
            return ctx.enter_context(nc.sbuf_tensor(name, shape, dt))

        def sem(name):
            return ctx.enter_context(nc.semaphore(name))

        w = sb("c_w", [P, KC, C])
        bo = sb("c_bo", [P, KC])
        bor = sb("c_bor", [P, KC])
        att = sb("c_att", [P, 2, KC, BANK])
        ps = [ctx.enter_context(nc.psum_tensor(f"c_ps{i}", [P, BANK], F32)) for i in range(8)]
        w_in = sem("c_w_in")
        x_in = sem("c_x_in")
        att_in = [sem(f"c_att_in{i}") for i in range(2)]
        scaled = sem("c_scaled")
        mm_done = sem("c_mm_done")
        added = sem("c_added")
        block = ctx.enter_context(nc.Block())

        @block.sync
        def _(sp):
            for s in (*att_in, mm_done, added):
                sp.sem_inc(s, CREDIT)
            sp.dma_start(w[:], woT.rearrange("(k p) o -> p k o", p=P)).then_inc(w_in, 16)
            sp.dma_start(bo[:], chan_o).then_inc(w_in, 16)
            with sp.Fori(0, CHUNKS // 2) as i:
                for b in range(2):
                    sp.wait_ge(mm_done, done((i * 2 + b) * KC - KC))
                    sp.dma_start(att[:, b, :, :], scr.att.rearrange("(k p) n -> p k n", p=P)[
                        :, :, bass.ds((i * 2 + b) * BANK, BANK)]).then_inc(att_in[b], 16)

        @block.gpsimd
        def _(pool):
            for k in range(KC):
                pool.dma_start(x1[:, k, :], x[k * P:(k + 1) * P, :]).then_inc(x_in, 16)

        @block.tensor
        def _(pe):
            pe.wait_ge(w_in, 32)
            with pe.Fori(0, CHUNKS // 2) as i:
                for b in range(2):
                    n = i * 2 + b
                    pe.wait_ge(att_in[b], done((i + 1) * 16))
                    for t in range(KC):
                        pe.wait_ge(added, done(n * KC + t + 1 - 8))
                        for k in range(KC):
                            mm = pe.matmul(ps[b * KC + t][:], w[:, k, t * P:(t + 1) * P], att[:, b, k, :],
                                           start=(k == 0), stop=(k == KC - 1))
                        mm.then_inc(mm_done, 1)

        @block.scalar
        def _(act):
            act.wait_ge(w_in, 32)
            act.mul(bor[:], bo[:], R2).then_inc(scaled, 1)
            act.wait_ge(scaled, 1)
            act.wait_ge(x_in, 16 * KC)
            for k in range(KC):
                act.activation(x1[:, k, :], x1[:, k, :], ACT.Identity, bias=bor[:, k:k + 1],
                               scale=R2).then_inc(scaled, 1)

        @block.vector
        def _(dve):
            dve.wait_ge(scaled, 1 + KC)
            with dve.Fori(0, CHUNKS // 2) as i:
                for b in range(2):
                    n = i * 2 + b
                    for t in range(KC):
                        dve.wait_ge(mm_done, done(n * KC + t + 1))
                        at = x1[:, t, bass.ds(n * BANK, BANK)]
                        dve.scalar_tensor_tensor(at, ps[b * KC + t][:], R2, at, ALU.mult,
                                                 ALU.add).then_inc(added, 1)


GH = 8
ROLES = 3
GROUPS = C // P
TAPS = 5
PAD = IMG + TAPS - 1
ROWS = BANK // IMG
HPG = P // GH
EPS_ATT = 1e-15


def stage_linear(nc, w_all, dw_all, pw_all, mask_d, heads_d, ident_d, scr, x1):
    DVE_CHUNKS = 6
    UNROLL = 2 * ROLES
    TURNS = GROUPS * ROLES // UNROLL
    RING = 3
    K, V, Q = range(ROLES)

    def order():
        out = []
        late = lambda t: [(t, 1, n) for n in range(DVE_CHUNKS)]
        for t in range(UNROLL):
            out += [(t, 0, n) for n in range(CHUNKS)]
            if t:
                out += late(t - 1)
            out += [(t, 1, n) for n in range(DVE_CHUNKS, CHUNKS)]
        return out + late(UNROLL - 1)

    PIECES = order()
    NP = len(PIECES)
    at = {piece: p for p, piece in enumerate(PIECES)}
    V_PIECES = [p for p in range(NP) if PIECES[p][0] % ROLES == V]
    last_piece = {(t, part): max(p for p, (a, b, _) in enumerate(PIECES) if (a, b) == (t, part))
                  for t in range(UNROLL) for part in range(2)}
    first_piece = {(t, part): min(p for p, (a, b, _) in enumerate(PIECES) if (a, b) == (t, part))
                   for t in range(UNROLL) for part in range(2)}

    with ExitStack() as ctx:
        def sb(name, shape, dt=F32):
            return ctx.enter_context(nc.sbuf_tensor(name, shape, dt))

        def pb(name):
            return ctx.enter_context(nc.psum_tensor(name, [P, BANK], F32))

        def sem(name):
            return ctx.enter_context(nc.semaphore(name))

        w = sb("d_w", [P, 2, KC, P])
        dw = sb("d_dw", [P, 2, TAPS * TAPS])
        pw = sb("d_pw", [P, 2, P])
        bd = sb("d_bd", [P, 2, P])
        wtap = sb("d_wtap", [P, TAPS * TAPS, P])
        ypad = sb("d_ypad", [P, 2, PAD, PAD])
        dsum = sb("d_dsum", [P, 2, DVE_CHUNKS * BANK])
        piece = sb("d_piece", [P, RING, BANK])
        tk = sb("d_tk", [P, 2, N // P, P])
        tv = sb("d_tv", [P, 2, 4, P + 1])
        vks = sb("d_vks", [P, P + 1])
        num_w = sb("d_num_w", [P, 2, P])
        den_w = sb("d_den_w", [P, 2, HPG])
        num = sb("d_num", [P, RING, BANK])
        den = sb("d_den", [HPG, RING, BANK])
        mask = sb("d_mask", [P, P])
        hmask = sb("d_hmask", [P, HPG])
        ident = sb("d_ident", [P, P])
        pmain = [pb(f"d_pmain{i}") for i in range(RING)]
        ptr = [pb(f"d_ptr{i}") for i in range(2)]
        pnum, pden, pvk = pb("d_pnum"), pb("d_pden"), pb("d_pvk")

        consts = sem("d_consts")
        zeroed = sem("d_zeroed")
        loaded = [sem(f"d_loaded{i}") for i in range(2)]
        built = sem("d_built")
        bd_made = sem("d_bd_made")
        main_done = sem("d_main_done")
        main_read = sem("d_main_read")
        post_done = sem("d_post_done")
        post_read = sem("d_post_read")
        vk_done = sem("d_vk_done")
        vk_read = sem("d_vk_read")
        vk_used = sem("d_vk_used")
        dlink = sem("d_dlink")
        stored = [sem(f"d_stored{i}") for i in range(RING)]
        TAPN = TAPS * TAPS

        block = ctx.enter_context(nc.Block())

        @block.sync
        def _(sp):
            for s in (*loaded, built, bd_made, main_done, main_read, post_done, post_read, vk_done,
                      vk_read, vk_used, dlink, *stored):
                sp.sem_inc(s, CREDIT)
            for dst, src in ((mask, mask_d), (hmask, heads_d), (ident, ident_d)):
                sp.dma_start(dst[:], src).then_inc(consts, 16)

            def load(i, t):
                tile, b = i * UNROLL + t, t % 2
                sp.wait_ge(dlink, done((i * UNROLL + t - 1) * TAPN))
                sp.wait_ge(built, done(i * UNROLL + t - 1))
                sp.dma_start(w[:, b, :, :], w_all[tile].rearrange("(k p) o -> p k o", p=P)).then_inc(loaded[b], 16)
                sp.dma_start(dw[:, b, :], dw_all[tile]).then_inc(loaded[b], 16)
                sp.dma_start(pw[:, b, :], pw_all[tile]).then_inc(loaded[b], 16)

            for dst, src in ((w[:, 0, :, :], w_all[0].rearrange("(k p) o -> p k o", p=P)),
                             (dw[:, 0, :], dw_all[0]), (pw[:, 0, :], pw_all[0])):
                sp.dma_start(dst, src).then_inc(loaded[0], 16)

            def turn(i, final):
                for p, (t, part, n) in enumerate(PIECES):
                    if t % ROLES == Q:
                        group = i * 2 + t // ROLES
                        sp.wait_ge(post_read, done(i * NP + p + 1))
                        sp.dma_start(scr.num[part, group, :, n * BANK:(n + 1) * BANK],
                                     num[:, p % RING, :]).then_inc(stored[p % RING], 16)
                        sp.dma_start(scr.den[part, group, :, n * BANK:(n + 1) * BANK],
                                     den[:, p % RING, :]).then_inc(stored[p % RING], 16)
                    if part == 0 and n == CHUNKS - 1 and not (final and t == UNROLL - 1):
                        load(i, t + 1)

            with sp.Fori(0, TURNS - 1) as i:
                turn(i, False)
            turn(TURNS - 1, True)
            for r in range(RING):
                mine = sum(t % ROLES == Q and p % RING == r for p, (t, _, _) in enumerate(PIECES))
                sp.wait_ge(stored[r], done(TURNS * mine * 32))

        @block.gpsimd
        def _(pool):
            pool.wait_ge(consts, 48)

            def build(i, t):
                b = t % 2
                pool.wait_ge(loaded[b], done((i * (UNROLL // 2) + t // 2 + 1) * 48))
                if t >= 2:
                    pool.wait_ge(main_done, done(i * NP + last_piece[t - 2, 1] + 1))
                else:
                    pool.wait_ge(main_done, done(i * NP))
                tile = i * UNROLL + t
                pool.tensor_tensor(bd[:, b, :], pw[:, b, :], mask[:], ALU.mult).then_inc(bd_made, 1)
                pool.wait_ge(bd_made, done(tile + 1))
                pool.wait_ge(main_done, done(i * NP + (at[t - 1, 1, CHUNKS - 1] + 1 if t else 0)))
                pool.tensor_tensor(wtap[:, 0, :], bd[:, b, :], dw[:, b, 0:1].to_broadcast([P, P]), ALU.mult)
                for tap in range(1, TAPN):
                    last = pool.tensor_scalar(wtap[:, tap, :], bd[:, b, :], dw[:, b, tap:tap + 1],
                                              None, ALU.mult)
                last.then_inc(built, 1)

            def blocks(i, g, part):
                count = (i * 2 + g) * 2 + part
                pool.wait_ge(vk_read, done(count + 1))
                t = g * ROLES + Q
                if g:
                    pool.wait_ge(post_done, done(i * NP + last_piece[t - ROLES, part] + 1))
                else:
                    pool.wait_ge(post_done, done(i * NP))
                pool.tensor_tensor(num_w[:, part, :], vks[:, 0:P], mask[:], ALU.mult)
                pool.tensor_scalar(den_w[:, part, :], hmask[:], vks[:, P:P + 1], None,
                                   ALU.mult).then_inc(vk_used, 1)

            with pool.Fori(0, TURNS) as i:
                for g in range(2):
                    build(i, g * ROLES + K)
                    build(i, g * ROLES + V)
                    blocks(i, g, 0)
                    build(i, g * ROLES + Q)
                    blocks(i, g, 1)

        @block.tensor
        def _(pe):
            pe.wait_ge(consts, 48)
            pe.wait_ge(zeroed, 4)

            def main(i, p):
                t, part, n = PIECES[p]
                b = t % 2
                tile = i * UNROLL + t
                pe.wait_ge(main_read, done(i * NP + p + 1 - RING))
                out = pmain[p % RING][:]
                if part == 0:
                    if n == 0:
                        pe.wait_ge(loaded[b], done((i * (UNROLL // 2) + t // 2 + 1) * 48))
                    for k in range(KC):
                        mm = pe.matmul(out, w[:, b, k, :], x1[:, k, n * BANK:(n + 1) * BANK],
                                       start=(k == 0), stop=(k == KC - 1))
                elif n >= DVE_CHUNKS:
                    if n == DVE_CHUNKS:
                        pe.wait_ge(built, done(tile + 1))
                        pe.wait_ge(main_read, done(i * NP + last_piece[t, 0] + 1))
                    for tap in range(TAPN):
                        dy, dx = tap // TAPS, tap % TAPS
                        mm = pe.matmul(out.rearrange("p (r c) -> p r c", c=IMG), wtap[:, tap, :],
                                       ypad[:, b, n * ROWS + dy:(n + 1) * ROWS + dy, dx:dx + IMG],
                                       start=(tap == 0), stop=(tap == TAPN - 1))
                else:
                    if n == 0:
                        pe.wait_ge(dlink, done((tile + 1) * TAPN))
                        pe.wait_ge(built, done(tile + 1))
                    mm = pe.matmul(out, bd[:, b, :], dsum[:, b, n * BANK:(n + 1) * BANK],
                                   start=True, stop=True)
                mm.then_inc(main_done, 1)

            def post(i, p):
                t, part, n = PIECES[p]
                role, group = t % ROLES, i * 2 + t // ROLES
                pe.wait_ge(main_read, done(i * NP + p + 1))
                if role == Q:
                    if p == first_piece[t, part]:
                        pe.wait_ge(vk_used, done(group * 2 + part + 1))
                    pe.wait_ge(post_read, done(i * NP + p))
                    pe.matmul(pnum[:], num_w[:, part, :], piece[:, p % RING, :], start=True, stop=True)
                    pe.matmul(pden[0:HPG, :], den_w[:, part, :], piece[:, p % RING, :], start=True,
                              stop=True).then_inc(post_done, 1)
                else:
                    pe.wait_ge(post_read, done(i * NP + p - 1))
                    for s in range(4):
                        tr = pe.transpose(ptr[p % 2][:, s * P:(s + 1) * P],
                                          piece[:, p % RING, s * P:(s + 1) * P], ident[:])
                    tr.then_inc(post_done, 1)

            def times_k(i, p):
                t, part, n = PIECES[p]
                if t % ROLES != V:
                    return
                pe.wait_ge(post_read, done(i * NP + p + 1))
                first, last = p == first_piece[t, part], p == last_piece[t, part]
                if first:
                    pe.wait_ge(vk_read, done((i * 2 + t // ROLES) * 2 + part))
                for s in range(4):
                    mm = pe.matmul(pvk[:, 0:P + 1], tk[:, part, n * 4 + s, :], tv[:, V_PIECES.index(p) % 2, s, :],
                                   start=(first and s == 0), stop=(last and s == 3))
                mm.then_inc(vk_done, 1)

            with pe.Fori(0, TURNS) as i:
                for p in range(NP + 2):
                    if p < NP:
                        main(i, p)
                    if p >= 2:
                        times_k(i, p - 2)
                    if 1 <= p <= NP:
                        post(i, p - 1)

        @block.scalar
        def _(act):
            act.wait_ge(zeroed, 4)

            def read_main(i, p):
                t, part, n = PIECES[p]
                b, role = t % 2, t % ROLES
                tile = i * UNROLL + t
                act.wait_ge(main_done, done(i * NP + p + 1))
                src = pmain[p % RING][:]
                if part == 0:
                    if n == 0:
                        if t:
                            act.wait_ge(dlink, done((tile - 1) * TAPN))
                        act.wait_ge(post_done, done(i * NP + (at[t - 2, 1, CHUNKS - 1] + 1 if t >= 2 else 0)))
                    act.activation(ypad[:, b, 2 + n * ROWS:2 + (n + 1) * ROWS, 2:2 + IMG],
                                   src.rearrange("p (r c) -> p r c", c=IMG), ACT.Copy)
                act.wait_ge(post_done, done(i * NP + p + 1 - RING))
                act.activation(piece[:, p % RING, :], src,
                               ACT.Copy if role == V else ACT.Relu).then_inc(main_read, 1)

            def read_post(i, p):
                t, part, n = PIECES[p]
                role, group = t % ROLES, i * 2 + t // ROLES
                act.wait_ge(post_done, done(i * NP + p + 1))
                if role == K:
                    if p == first_piece[t, part]:
                        act.wait_ge(vk_read, done((group - 1) * 2 + part + 1))
                    act.activation(tk[:, part, n * 4:(n + 1) * 4, :],
                                   ptr[p % 2][:].rearrange("p (s c) -> p s c", c=P),
                                   ACT.Copy).then_inc(post_read, 1)
                elif role == V:
                    k = V_PIECES.index(p)
                    act.wait_ge(vk_done, done(i * len(V_PIECES) + k - 1))
                    act.activation(tv[:, k % 2, :, 0:P], ptr[p % 2][:].rearrange("p (s c) -> p s c", c=P),
                                   ACT.Copy).then_inc(post_read, 1)
                else:
                    r = p % RING
                    mine = [x for x in range(NP) if PIECES[x][0] % ROLES == Q and x % RING == r]
                    act.wait_ge(stored[r], done((i * len(mine) + mine.index(p)) * 32))
                    act.activation(num[:, r, :], pnum[:], ACT.Copy)
                    act.activation(den[:, r, :], pden[0:HPG, :], ACT.Copy, bias=EPS_ATT).then_inc(post_read, 1)

            def read_vk(i, p):
                t, part, _ = PIECES[p]
                if t % ROLES == V and p == last_piece[t, part]:
                    count = (i * 2 + t // ROLES) * 2 + part
                    act.wait_ge(vk_done, done(i * len(V_PIECES) + V_PIECES.index(p) + 1))
                    act.wait_ge(vk_used, done(count))
                    act.activation(vks[:], pvk[:, 0:P + 1], ACT.Copy).then_inc(vk_read, 1)

            with act.Fori(0, TURNS) as i:
                for p in range(NP + 2):
                    if p < NP:
                        read_main(i, p)
                    if p >= 2:
                        read_vk(i, p - 2)
                    if 1 <= p <= NP:
                        read_post(i, p - 1)

        @block.vector
        def _(dve):
            for b in range(2):
                dve.memset(ypad[:, b, :, :], 0.0).then_inc(zeroed, 1)
                dve.memset(tv[:, b, :, P:P + 1], 1.0).then_inc(zeroed, 1)
            with dve.Fori(0, TURNS) as i:
                for t in range(UNROLL):
                    b = t % 2
                    tile = i * UNROLL + t
                    dve.wait_ge(loaded[b], done((i * (UNROLL // 2) + t // 2 + 1) * 48))
                    dve.wait_ge(main_read, done(i * NP + last_piece[t, 0] + 1))
                    dve.wait_ge(main_done, done(i * NP + (at[t - 2, 1, DVE_CHUNKS - 1] + 1 if t >= 2 else 0)))
                    acc = dsum[:, b, :].rearrange("p (r c) -> p r c", c=IMG)
                    for tap in range(TAPN):
                        dy, dx = tap // TAPS, tap % TAPS
                        src = ypad[:, b, dy:dy + DVE_CHUNKS * ROWS, dx:dx + IMG]
                        if tap == 0:
                            add = dve.tensor_scalar(acc, src, dw[:, b, tap:tap + 1], None, ALU.mult)
                        else:
                            dve.wait_ge(dlink, done(tile * TAPN + tap))
                            add = dve.scalar_tensor_tensor(acc, src, dw[:, b, tap:tap + 1], acc,
                                                           ALU.mult, ALU.add)
                        add.then_inc(dlink, 1)


def stage_project(nc, wprojT, chan_bn, scr, x1, out):
    BN_EPS = 1e-5
    MS = 2 * GROUPS
    HALF = N // 2
    with ExitStack() as ctx:
        def sb(name, shape, dt=F32):
            return ctx.enter_context(nc.sbuf_tensor(name, shape, dt))

        def sem(name):
            return ctx.enter_context(nc.semaphore(name))

        w = sb("f_w", [P, MS, C])
        par = sb("f_par", [P, KC, 2])
        num = sb("f_num", [P, 2, MS, BANK])
        rden = sb("f_rden", [P, 2, GROUPS, BANK])
        proj = sb("f_proj", [P, KC, N])
        stats = sb("f_stats", [P, KC, CHUNKS, 6])
        mv = sb("f_mv", [P, KC, 2])
        coef = sb("f_coef", [P, 2, KC])
        var = sb("f_var", [P, KC])
        sd = sb("f_sd", [P, KC])
        rstd = sb("f_rstd", [P, KC])
        tmp = sb("f_tmp", [P, KC])
        ps = [ctx.enter_context(nc.psum_tensor(f"f_ps{i}", [P, BANK], F32)) for i in range(8)]

        den_in = sem("f_den_in")
        inverted = sem("f_inverted")
        inv_out = sem("f_inv_out")
        w_in = sem("f_w_in")
        num_in = [sem(f"f_num_in{i}") for i in range(2)]
        rden_in = [sem(f"f_rden_in{i}") for i in range(2)]
        divided = sem("f_divided")
        mm_done = sem("f_mm_done")
        copied = sem("f_copied")
        measured = sem("f_measured")
        link_s = sem("f_link")
        var_ready = sem("f_var_ready")
        root = sem("f_root")
        coef_ready = sem("f_coef_ready")
        scaled = sem("f_scaled")
        summed = sem("f_summed")
        stored = sem("f_stored")
        block = ctx.enter_context(nc.Block())

        @block.sync
        def _(sp):
            for s in (*num_in, *rden_in, divided, mm_done, copied, measured):
                sp.sem_inc(s, CREDIT)
            sp.dma_start(proj[:, 0, :], scr.den.rearrange("a g h n -> (a g h) n")).then_inc(den_in, 16)
            sp.dma_start(w[:], wprojT.rearrange("(m p) o -> p m o", p=P)).then_inc(w_in, 16)
            sp.dma_start(par[:], chan_bn).then_inc(w_in, 16)
            sp.wait_ge(inverted, 1)
            sp.dma_start(scr.rden, proj[:, 1, :]).then_inc(inv_out, 16)
            sp.wait_ge(inv_out, 16)
            with sp.Fori(0, CHUNKS // 2) as i:
                for b in range(2):
                    n = i * 2 + b
                    at = bass.ds(n * BANK, BANK)
                    sp.wait_ge(mm_done, done(n * KC - KC))
                    sp.dma_start(num[:, b, :, :], scr.num.rearrange("a g p n -> p (a g) n")[
                        :, :, at]).then_inc(num_in[b], 16)
                    for part in range(2):
                        sp.wait_ge(divided, done(n * 2 + part - 1))
                        for g in range(GROUPS):
                            row = (part * GROUPS + g) * HPG
                            sp.dma_start(rden[:, part, g, :], scr.rden[row:row + HPG, at].unsqueeze(1)
                                         .to_broadcast([HPG, GH, BANK])).then_inc(rden_in[part], 16)
            for t in range(KC):
                for h in range(2):
                    sp.wait_ge(summed, t * 2 + h + 1)
                    sp.dma_start(out[t * P:(t + 1) * P, h * HALF:(h + 1) * HALF],
                                 proj[:, t, h * HALF:(h + 1) * HALF]).then_inc(stored, 16)
            sp.wait_ge(stored, KC * 2 * 16)

        @block.tensor
        def _(pe):
            pe.wait_ge(w_in, 32)
            with pe.Fori(0, CHUNKS // 2) as i:
                for b in range(2):
                    n = i * 2 + b
                    for t in range(KC):
                        if t == 0:
                            pe.wait_ge(divided, done(n * 2 + 2))
                        pe.wait_ge(copied, done(n * KC + t + 1 - 8))
                        for m in range(MS):
                            mm = pe.matmul(ps[b * KC + t][:], w[:, m, t * P:(t + 1) * P], num[:, b, m, :],
                                           start=(m == 0), stop=(m == MS - 1))
                        mm.then_inc(mm_done, 1)

        @block.scalar
        def _(act):
            act.wait_ge(inv_out, 16)
            with act.Fori(0, CHUNKS // 2) as i:
                for b in range(2):
                    n = i * 2 + b
                    for t in range(KC):
                        act.wait_ge(mm_done, done(n * KC + t + 1))
                        act.activation(proj[:, t, bass.ds(n * BANK, BANK)], ps[b * KC + t][:],
                                       ACT.Copy).then_inc(copied, 1)
            act.wait_ge(var_ready, 1)
            act.activation(sd[:], var[:], ACT.Sqrt).then_inc(root, 1)
            act.wait_ge(coef_ready, 1)
            for t in range(KC):
                for h in range(2):
                    at = proj[:, t, h * HALF:(h + 1) * HALF]
                    act.activation(at, at, ACT.Identity, bias=coef[:, 1, t:t + 1],
                                   scale=coef[:, 0, t:t + 1]).then_inc(scaled, 1)

        @block.vector
        def _(dve):
            links = 0

            def link(ins):
                nonlocal links
                links += 1
                ins.then_inc(link_s, 1)
                dve.wait_ge(link_s, links)

            dve.wait_ge(den_in, 16)
            dve.reciprocal(proj[:, 1, :], proj[:, 0, :]).then_inc(inverted, 1)

            def divide(n, b):
                for part in range(2):
                    if part == 0:
                        dve.wait_ge(num_in[b], done(16 * (n // 2 + 1)))
                    dve.wait_ge(rden_in[part], done(64 * (n + 1)))
                    at = num[:, b, part * GROUPS:(part + 1) * GROUPS, :]
                    dve.tensor_tensor(at, at, rden[:, part, :, :], ALU.mult).then_inc(divided, 1)

            def measure(n):
                for t in range(KC):
                    dve.wait_ge(copied, done(n * KC + t + 1))
                    dve.bn_stats(stats[:, t, n, :], proj[:, t, n * BANK:(n + 1) * BANK]).then_inc(measured, 1)

            divide(0, 0)
            for n in range(CHUNKS):
                if n + 1 < CHUNKS:
                    divide(n + 1, (n + 1) % 2)
                measure(n)
            dve.wait_ge(w_in, 32)
            dve.wait_ge(measured, done(KC * CHUNKS))
            for t in range(KC):
                last = dve.bn_aggr(mv[:, t, :], stats[:, t, :, :].rearrange("p j s -> p (j s)"))
            link(last)
            dve.tensor_scalar(var[:], mv[:, :, 1], BN_EPS, None, ALU.add).then_inc(var_ready, 1)
            dve.wait_ge(root, 1)
            link(dve.reciprocal(rstd[:], sd[:]))
            link(dve.tensor_tensor(tmp[:], rstd[:], rstd[:], ALU.mult))
            link(dve.tensor_tensor(tmp[:], tmp[:], var[:], ALU.mult))
            link(dve.tensor_scalar(tmp[:], tmp[:], -0.5, 1.5, ALU.mult, ALU.add))
            link(dve.tensor_tensor(rstd[:], rstd[:], tmp[:], ALU.mult))
            link(dve.tensor_tensor(coef[:, 0, :], rstd[:], par[:, :, 0], ALU.mult))
            link(dve.tensor_tensor(tmp[:], mv[:, :, 0], coef[:, 0, :], ALU.mult))
            dve.tensor_tensor(coef[:, 1, :], par[:, :, 1], tmp[:], ALU.subtract).then_inc(coef_ready, 1)
            for t in range(KC):
                for h in range(2):
                    dve.wait_ge(scaled, t * 2 + h + 1)
                    at = slice(h * HALF, (h + 1) * HALF)
                    dve.tensor_tensor(proj[:, t, at], proj[:, t, at], x1[:, t, at], ALU.add).then_inc(summed, 1)


def conv_seq(nc, x, chan, wqT, wkT, wvT, bv, bo, woT, w_all, dw_all, pw_all, wprojT, chan_bn,
             group_mean, mask, hmask, ident, out):
    scr = Scratch(nc)
    with nc.sbuf_tensor("v_tok", [P, N // P, C], F32) as v_tok:
        stage_qkv(nc, x, chan, wqT, wkT, wvT, bv, group_mean, scr, v_tok)
        stage_attention(nc, scr, v_tok, ident)
    with nc.sbuf_tensor("x1", [P, KC, N], F32) as x1:
        stage_output(nc, x, bo, woT, scr, x1)
        stage_linear(nc, w_all, dw_all, pw_all, mask, hmask, ident, scr, x1)
        stage_project(nc, wprojT, chan_bn, scr, x1, out)


def kernel(**inputs):
    import numpy as np
    import concourse.bacc as bacc
    from concourse.bass_utils import run_bass_kernel_spmd as run

    def by_channel(*vectors):
        return np.stack([np.asarray(v).reshape(KC, P) for v in vectors], -1).transpose(1, 0, 2)

    a = {n: np.asarray(v) for n, v in inputs.items()}
    l0 = {n[len("L0_conv_"):]: v for n, v in a.items() if n.startswith("L0_conv_")}
    l1 = {n[len("L1_conv_"):]: v for n, v in a.items() if n.startswith("L1_conv_")}
    roles = [1, 2, 0]
    w_all = l1["w_qkv"].reshape(GROUPS, HPG, ROLES, GH, C)[:, :, roles].transpose(0, 2, 4, 1, 3)
    dw_all = l1["w_dw"].reshape(GROUPS, HPG, ROLES, GH, TAPS * TAPS)[:, :, roles].transpose(0, 2, 1, 3, 4)
    pw = l1["w_pw"].reshape(GROUPS, HPG, ROLES, GH, GH)[:, :, roles].transpose(0, 2, 1, 4, 3)
    pw_all = np.tile(pw.reshape(GROUPS * ROLES, P, GH), (1, 1, HPG))
    eye = np.eye(P, dtype=np.float32)
    arrays = {
        "x": a["x"].reshape(C, N),
        "chan": by_channel(l0["gn_w"], l0["gn_b"], l0["bq"], l0["bk"]),
        "wqT": l0["wq"].T, "wkT": l0["wk"].T, "wvT": l0["wv"].T, "bv": l0["bv"],
        "bo": by_channel(l0["bo"])[:, :, 0],
        "woT": l0["wo"].T,
        "w_all": w_all.reshape(GROUPS * ROLES, C, P),
        "dw_all": dw_all.reshape(GROUPS * ROLES, P, TAPS * TAPS),
        "pw_all": pw_all,
        "wprojT": l1["w_proj"].T,
        "chan_bn": by_channel(l1["bn_gamma"], l1["bn_beta"]),
        "group_mean": np.kron(np.eye(P // GN_GROUP), np.full((GN_GROUP, GN_GROUP), 1.0 / GN_GROUP)).astype(np.float32),
        "mask": np.kron(np.eye(HPG), np.ones((GH, GH))).astype(np.float32),
        "hmask": np.kron(np.eye(HPG), np.ones((GH, 1))).astype(np.float32),
        "ident": eye,
    }
    nc = bacc.Bacc("TRN2", target_bir_lowering=False, num_devices=1)
    args, ins = [], {}
    for name, v in arrays.items():
        v = np.ascontiguousarray(v)
        ins[f"in_{name}"] = v
        args.append(nc.dram_tensor(f"in_{name}", v.shape, mybir.dt.from_np(v.dtype), kind="ExternalInput").ap())
    out = nc.dram_tensor("out_0", (1, C, IMG, IMG), F32, kind="ExternalOutput").ap()
    conv_seq(nc, *args, out.rearrange("b c h w -> (b c) (h w)"))
    r = run(nc, [ins], core_ids=[0])
    return r.results[0]["out_0"]
```

```python
from contextlib import ExitStack

import concourse.bass as bass
from concourse import mybir

F32 = mybir.dt.float32
F32R = mybir.dt.float32r
ALU = mybir.AluOpType
ACT = mybir.ActivationFunctionType
AX = mybir.AxisListType

P = 128
C = 512
IMG = 64
N = IMG * IMG
KC = C // P
BANK = 512
CHUNKS = N // BANK

GN_GROUP = 16
GN_EPS = 1e-6
HEADS = 16
HD = C // HEADS
SCALE = float(HD) ** -0.5

CREDIT = 8


def done(n):
    return n + CREDIT


class Scratch:

    def __init__(self, nc):
        self.qh = nc.dram_tensor("scratch_qh", (C, N), F32, kind="Internal").ap()
        self.ql = nc.dram_tensor("scratch_ql", (C, N), F32, kind="Internal").ap()
        self.kh = nc.dram_tensor("scratch_kh", (C, N), F32, kind="Internal").ap()
        self.kl = nc.dram_tensor("scratch_kl", (C, N), F32, kind="Internal").ap()
        self.num = nc.dram_tensor("scratch_num", (2, GROUPS, P, N), F32, kind="Internal").ap()
        self.den = nc.dram_tensor("scratch_den", (2, GROUPS, HPG, N), F32, kind="Internal").ap()
        self.rden = nc.dram_tensor("scratch_rden", (2 * GROUPS * HPG, N), F32, kind="Internal").ap()
        self.att = nc.dram_tensor("scratch_att", (HEADS, 2, HD, N), F32, kind="Internal").ap()
        self.att_den = nc.dram_tensor("scratch_att_den", (HEADS, 2, N), F32, kind="Internal").ap()
        self.att_rden = nc.dram_tensor("scratch_att_rden", (HEADS, N), F32, kind="Internal").ap()


def stage_qkv(nc, x, chan, wqT, wkT, wvT, bv, group_mean, scr, v_tok):
    with ExitStack() as ctx:
        def sb(name, shape, dt=F32):
            return ctx.enter_context(nc.sbuf_tensor(name, shape, dt))

        def sem(name):
            return ctx.enter_context(nc.semaphore(name))

        xs = sb("a_x", [P, KC, N])
        w = {r: sb(f"a_w{r}", [P, KC, C]) for r in "qkv"}
        par = sb("a_par", [P, KC, 4])
        bv_rows = sb("a_bv_rows", [P, C])
        gmean = sb("a_gmean", [P, P])
        stats = sb("a_stats", [P, KC, CHUNKS, 6])
        mv = sb("a_mv", [P, KC, 2])
        dev = sb("a_dev", [P, KC])
        spread = sb("a_spread", [P, KC])
        mean = sb("a_mean", [P, KC])
        rstd = sb("a_rstd", [P, KC])
        tmp = sb("a_tmp", [P, KC])
        var = sb("a_var", [P, KC])
        sd = sb("a_sd", [P, KC])
        aff = sb("a_aff", [P, 2, 2, KC])
        vn = sb("a_vn", [P, 2, KC, BANK])
        high = sb("a_high", [P, 2, 4, BANK], F32R)
        low = sb("a_low", [P, 2, 4, BANK], F32R)
        ps = [ctx.enter_context(nc.psum_tensor(f"a_ps{i}", [P, BANK], F32)) for i in range(8)]

        x_in = sem("a_x_in")
        par_in = sem("a_par_in")
        w_in = sem("a_w_in")
        stat = sem("a_stat")
        moments = sem("a_moments")
        spread_ready = sem("a_spread_ready")
        gsum = sem("a_gsum")
        var_ready = sem("a_var_ready")
        root = sem("a_root")
        coef = sem("a_coef")
        qn_ready = sem("a_qn_ready")
        vn_ready = sem("a_vn_ready")
        mm_done = sem("a_mm_done")
        high_done = sem("a_high_done")
        low_done = sem("a_low_done")
        v_done = sem("a_v_done")
        stored = [sem(f"a_stored_{r}") for r in "qk"]

        TILES = 12
        block = ctx.enter_context(nc.Block())

        @block.sync
        def _(sp):
            for k in range(KC):
                sp.dma_start(xs[:, k, :], x[k * P:(k + 1) * P, :]).then_inc(x_in, 16)
            sp.dma_start(par[:], chan).then_inc(par_in, 16)
            sp.dma_start(gmean[:], group_mean).then_inc(par_in, 16)
            sp.dma_start(bv_rows[:], bv.partition_broadcast(P)).then_inc(par_in, 16)
            for r, src in (("q", wqT), ("k", wkT), ("v", wvT)):
                sp.dma_start(w[r][:], src.rearrange("(k p) o -> p k o", p=P)).then_inc(w_in, 16)
            with sp.Fori(0, CHUNKS // 2) as i:
                for b in range(2):
                    n = i * 2 + b
                    for r, (hi_d, lo_d) in enumerate(((scr.qh, scr.ql), (scr.kh, scr.kl))):
                        sp.wait_ge(low_done, done(n * 8 + 4 * r + 4))
                        for dst, src in ((hi_d, high), (lo_d, low)):
                            sp.dma_start(
                                dst.rearrange("(k p) n -> p k n", p=P)[:, :, bass.ds(n * BANK, BANK)],
                                src[:, r, :, :].bitcast(F32)).then_inc(stored[r], 16)
            for s in stored:
                sp.wait_ge(s, done(CHUNKS * 2 * 16))

        @block.vector
        def _(dve):
            for s in (low_done, v_done):
                dve.sem_inc(s, CREDIT)
            links = 0

            def link(ins):
                nonlocal links
                links += 1
                ins.then_inc(stat, 1)
                dve.wait_ge(stat, links)

            for k in range(KC):
                dve.wait_ge(x_in, 16 * KC)
                for j in range(CHUNKS):
                    last = dve.bn_stats(stats[:, k, j, :], xs[:, k, j * BANK:(j + 1) * BANK])
            link(last)
            for k in range(KC):
                last = dve.bn_aggr(mv[:, k, :], stats[:, k, :, :].rearrange("p j s -> p (j s)"))
            link(last)
            dve.wait_ge(par_in, 16 * 3)

            def affine(norm):
                dve.sem_inc(moments, 1)
                dve.wait_ge(gsum, 2 * norm + 1)
                link(dve.tensor_copy(mean[:], ps[0][:, 0:KC]))
                link(dve.tensor_tensor(dev[:], mv[:, :, 0], mean[:], ALU.subtract))
                link(dve.tensor_tensor(dev[:], dev[:], dev[:], ALU.mult))
                dve.tensor_tensor(spread[:], dev[:], mv[:, :, 1], ALU.add).then_inc(spread_ready, 1)
                dve.wait_ge(gsum, 2 * norm + 2)
                dve.tensor_scalar(var[:], ps[1][:, 0:KC], GN_EPS, None, ALU.add).then_inc(var_ready, 1)
                dve.wait_ge(root, norm + 1)
                link(dve.reciprocal(rstd[:], sd[:]))
                link(dve.tensor_tensor(tmp[:], rstd[:], rstd[:], ALU.mult))
                link(dve.tensor_tensor(tmp[:], tmp[:], var[:], ALU.mult))
                link(dve.tensor_scalar(tmp[:], tmp[:], -0.5, 1.5, ALU.mult, ALU.add))
                link(dve.tensor_tensor(rstd[:], rstd[:], tmp[:], ALU.mult))
                link(dve.tensor_tensor(aff[:, norm, 0, :], rstd[:], par[:, :, 0], ALU.mult))
                link(dve.tensor_tensor(tmp[:], mean[:], aff[:, norm, 0, :], ALU.mult))
                return dve.tensor_tensor(aff[:, norm, 1, :], par[:, :, 1], tmp[:], ALU.subtract)

            link(affine(0))
            link(dve.tensor_tensor(tmp[:], mv[:, :, 0], aff[:, 0, 0, :], ALU.mult))
            link(dve.tensor_tensor(mv[:, :, 0], tmp[:], aff[:, 0, 1, :], ALU.add))
            link(dve.tensor_tensor(tmp[:], mv[:, :, 1], aff[:, 0, 0, :], ALU.mult))
            link(dve.tensor_tensor(mv[:, :, 1], tmp[:], aff[:, 0, 0, :], ALU.mult))
            link(affine(1))
            dve.sem_inc(coef, 1)
            for k in range(KC):
                dve.tensor_scalar(xs[:, k, :], xs[:, k, :], aff[:, 0, 0, k:k + 1],
                                  aff[:, 0, 1, k:k + 1], ALU.mult, ALU.add).then_inc(qn_ready, 1)

            with dve.Fori(0, CHUNKS // 2) as i:
                for b in range(2):
                    n = i * 2 + b
                    for m in range(8):
                        r, t = m // 4, m % 4
                        g = b * TILES + m
                        dve.wait_ge(high_done, done(n * 8 + m + 1))
                        if t == 0:
                            dve.wait_ge(stored[r], done(n * 32))
                        bias = par[:, t, 2 + r:3 + r]
                        dve.scalar_tensor_tensor(low[:, r, t, :], ps[g % 8][:], bias,
                                                 high[:, r, t, :].bitcast(F32), ALU.add,
                                                 ALU.subtract).then_inc(low_done, 1)
                    for t in range(4):
                        g = b * TILES + 8 + t
                        dve.wait_ge(mm_done, done(n * TILES + 8 + t + 1))
                        dve.tensor_tensor(v_tok[:, n * 4 + t, :], ps[g % 8][:], bv_rows[:],
                                          ALU.add).then_inc(v_done, 1)

        @block.scalar
        def _(act):
            act.sem_inc(high_done, CREDIT)
            act.sem_inc(vn_ready, CREDIT)
            for norm in range(2):
                act.wait_ge(var_ready, norm + 1)
                act.activation(sd[:], var[:], ACT.Sqrt).then_inc(root, 1)
            act.wait_ge(coef, 1)
            act.wait_ge(qn_ready, KC)

            def normalise(n, b):
                for k in range(KC):
                    last = act.activation(vn[:, b, k, :], xs[:, k, bass.ds(n * BANK, BANK)], ACT.Identity,
                                          bias=aff[:, 1, 1, k:k + 1], scale=aff[:, 1, 0, k:k + 1])
                last.then_inc(vn_ready, 1)

            def pair(i, final):
                for b in range(2):
                    n = i * 2 + b
                    if not (final and b == 1):
                        act.wait_ge(mm_done, done(n * TILES))
                        normalise(n + 1, 1 - b)
                    for m in range(8):
                        r, t = m // 4, m % 4
                        g = b * TILES + m
                        act.wait_ge(mm_done, done(n * TILES + m + 1))
                        if t == 0:
                            act.wait_ge(stored[r], done(n * 32))
                            act.wait_ge(low_done, done(n * 8))
                        act.activation(high[:, r, t, :], ps[g % 8][:], ACT.Identity,
                                       bias=par[:, t, 2 + r:3 + r]).then_inc(high_done, 1)

            normalise(0, 0)
            with act.Fori(0, CHUNKS // 2 - 1) as i:
                pair(i, False)
            pair(CHUNKS // 2 - 1, True)

        @block.tensor
        def _(pe):
            for s in (mm_done, *stored):
                pe.sem_inc(s, CREDIT)
            pe.wait_ge(par_in, 16 * 3)
            for norm in range(2):
                pe.wait_ge(moments, norm + 1)
                pe.matmul(ps[0][:, 0:KC], gmean[:], mv[:, :, 0], start=True, stop=True).then_inc(gsum, 1)
                pe.wait_ge(spread_ready, norm + 1)
                pe.matmul(ps[1][:, 0:KC], gmean[:], spread[:], start=True, stop=True).then_inc(gsum, 1)
            pe.wait_ge(qn_ready, KC)
            pe.wait_ge(w_in, 16 * 3)
            with pe.Fori(0, CHUNKS // 2) as i:
                for b in range(2):
                    n = i * 2 + b
                    for m in range(TILES):
                        g = b * TILES + m
                        if m == 0:
                            pe.wait_ge(v_done, done(n * 4))
                        if m == 4:
                            pe.wait_ge(vn_ready, done(n + 1))
                        if m < 4:
                            pe.wait_ge(low_done, done(n * 8))
                        elif m >= 8:
                            pe.wait_ge(low_done, done(n * 8 + m - 8 + 1))
                        r, t = m // 4, m % 4
                        for k in range(KC):
                            if r == 0:
                                lhs, rhs = w["q"][:, k, t * P:(t + 1) * P], xs[:, k, bass.ds(n * BANK, BANK)]
                            elif r == 1:
                                lhs, rhs = w["k"][:, k, t * P:(t + 1) * P], vn[:, b, k, :]
                            else:
                                lhs, rhs = vn[:, b, k, t * P:(t + 1) * P], w["v"][:, k, :]
                            last = pe.matmul(ps[g % 8][:], lhs, rhs, start=(k == 0), stop=(k == KC - 1))
                        last.then_inc(mm_done, 1)


def stage_attention(nc, scr, v_tok, ident_d):
    UNIT = 1024
    UNITS = N // UNIT
    KT = N // P
    PAIRS = KT // 2
    OCT = 8
    OCTS = KT // OCT
    ADDS = 5
    SUMS = 3 * HD
    FULL = SUMS + 2
    QT = UNIT // P
    MAXES = QT * CHUNKS
    SLOTS = MAXES + 1
    HEADS_PER_TURN = 2
    TURN = HEADS_PER_TURN * UNITS
    TURNS = HEADS // HEADS_PER_TURN
    ALL = HEADS * UNITS
    PBUF = 2 * OCT
    with ExitStack() as ctx:
        def sb(name, shape, dt=F32):
            return ctx.enter_context(nc.sbuf_tensor(name, shape, dt))

        def pb(name, shape):
            return ctx.enter_context(nc.psum_tensor(name, shape, F32))

        def sem(name):
            return ctx.enter_context(nc.semaphore(name))

        kst = sb("b_kst", [P, 2, N], F32R)
        qst = sb("b_qst", [P, 2, UNIT], F32R)
        vst = sb("b_vst", [P, 2, KT, HD])
        prob = sb("b_prob", [P, PBUF, UNIT])
        sums = sb("b_sums", [P, 2, 2, UNIT])
        ones = sb("b_ones", [P, 1])
        mx = sb("b_mx", [P, QT, CHUNKS])
        mtop = sb("b_mtop", [P, QT])
        mneg = sb("b_mneg", [P, 2 * QT])
        mrow = sb("b_mrow", [2 * QT, P], F32R)
        outn = sb("b_outn", [P, BANK])
        outd = sb("b_outd", [P, BANK])
        ident = sb("b_ident", [P, P])
        pscore = [pb(f"b_pscore{i}", [P, UNIT]) for i in range(2)]
        pmax = [pb(f"b_pmax{i}", [P, BANK]) for i in range(2)]
        pout = pb("b_pout", [P, BANK])
        pden = pb("b_pden", [P, BANK])

        consts = sem("b_consts")
        k_in = [sem(f"b_k_in{i}") for i in range(2)]
        q_in = [sem(f"b_q_in{i}") for i in range(2)]
        v_in = sem("b_v_in")
        shift_in = sem("b_shift_in")
        scored = sem("b_scored")
        exped = sem("b_exped")
        times_v_done = sem("b_times_v_done")
        dve_added = sem("b_dve_added")
        pool_added = sem("b_pool_added")
        den_done = sem("b_den_done")
        max_mm = sem("b_max_mm")
        max_read = sem("b_max_read")
        mlink = sem("b_mlink")
        packed = sem("b_packed")
        out_read = sem("b_out_read")
        den_read = sem("b_den_read")
        out_stored = sem("b_out_stored")
        den_stored = sem("b_den_stored")
        counted = (*k_in, *q_in, v_in, shift_in, scored, exped, times_v_done, dve_added, pool_added,
                   den_done, max_mm, max_read, mlink, packed, out_read, den_read, out_stored,
                   den_stored)

        heads = {n: a.rearrange("(h d) n -> h d n", d=HD) for n, a in
                 (("qh", scr.qh), ("ql", scr.ql), ("kh", scr.kh), ("kl", scr.kl))}
        block = ctx.enter_context(nc.Block())

        def units(i):
            for par in range(HEADS_PER_TURN):
                for c in range(UNITS):
                    head = i * HEADS_PER_TURN + par
                    yield head * UNITS + c, head, par, c

        @block.sync
        def _(sp):
            for s in counted:
                sp.sem_inc(s, CREDIT)
            sp.dma_start(ident[:], ident_d).then_inc(consts, 16)

            def load_k(head, par):
                for row, name in ((0, "kh"), (HD, "kl"), (2 * HD, "kh")):
                    sp.dma_start(kst[row:row + HD, par, :].bitcast(F32), heads[name][head]).then_inc(k_in[par], 16)

            def load_q(head, c, b):
                for row, name in ((0, "qh"), (HD, "qh"), (2 * HD, "ql")):
                    sp.dma_start(qst[row:row + HD, b, :].bitcast(F32),
                                 heads[name][head, :, c * UNIT:(c + 1) * UNIT]).then_inc(q_in[b], 16)

            def load_shift(u, b):
                sp.wait_ge(max_read, done((u + 1) * SLOTS))
                for half in range(2):
                    sp.dma_start(qst[SUMS + half:SUMS + half + 1, b, :].bitcast(F32).rearrange(
                        "o (t j) -> o t j", j=P),
                        mrow[half * QT:(half + 1) * QT, :].bitcast(F32)).then_inc(shift_in, 16)

            def store(u, head, c):
                sp.wait_ge(out_read, done(u + 1))
                for half in (1, 0):
                    at = c * UNIT + half * BANK
                    sp.dma_start(scr.att[head, :, :, at:at + BANK],
                                 outn[half * 2 * HD:(half + 1) * 2 * HD, :]).then_inc(out_stored, 16)
                sp.wait_ge(den_read, done(u + 1))
                for half in (1, 0):
                    at = c * UNIT + half * BANK
                    sp.dma_start(scr.att_den[head, :, at:at + BANK],
                                 outd[half * 2 * HD:(half + 1) * 2 * HD:HD, :]).then_inc(den_stored, 16)

            load_k(0, 0)
            load_q(0, 0, 0)
            load_q(0, 1, 1)
            load_k(1, 1)
            load_shift(0, 0)

            def turn(i, first, final):
                for u, head, par, c in units(i):
                    if not (first and par == c == 0):
                        store(u - 1, head if c else head - 1, (c - 1) % UNITS)
                    if not (final and par * UNITS + c == TURN - 1):
                        load_shift(u + 1, (c + 1) % 2)
                    sp.wait_ge(scored, done((u + 1) * KT))
                    nxt = par * UNITS + c + 2
                    if not (final and nxt >= TURN):
                        load_q(i * HEADS_PER_TURN + nxt // UNITS, nxt % UNITS, c % 2)
                    if c == UNITS - 1 and not final:
                        load_k(head + HEADS_PER_TURN, par)

            turn(0, True, False)
            with sp.Fori(1, TURNS - 1) as i:
                turn(i, False, False)
            turn(TURNS - 1, False, True)
            store(ALL - 1, HEADS - 1, UNITS - 1)
            sp.wait_ge(out_stored, done(ALL * 32))
            sp.wait_ge(den_stored, done(ALL * 32))

        @block.gpsimd
        def _(pool):
            def eight_steps(g, b):
                p = prob[:, b * OCT:(b + 1) * OCT, :]
                a_, b_ = sums[:, b, 0, :], sums[:, b, 1, :]
                pool.wait_ge(den_done, done(g - 1))
                pool.wait_ge(exped, done(g * OCT + 2))
                pool.tensor_tensor(a_, p[:, 0, :], p[:, 1, :], ALU.add).then_inc(pool_added, 1)
                for n, (acc, step) in enumerate(((a_, 2), (a_, 3), (b_, 6), (b_, 7))):
                    pool.wait_ge(pool_added, done(g * ADDS + n + 1))
                    pool.wait_ge(exped, done(g * OCT + step + 1))
                    if n == 2:
                        pool.wait_ge(dve_added, done(g + 1))
                    pool.tensor_tensor(acc, acc, p[:, step, :], ALU.add).then_inc(pool_added, 1)

            with pool.Fori(0, ALL * OCTS // 2) as j:
                for b in range(2):
                    eight_steps(j * 2 + b, b)

        def slots(pair, place):
            room = PAIRS - 2
            mine = [m for m in range(MAXES) if m * room // MAXES == pair]
            return (mine[0:2], mine[2:4], mine[4:])[place]

        @block.tensor
        def _(pe):
            pe.wait_ge(consts, 16 + 3)

            def max_product(u, m, par, b):
                t, j = m // CHUNKS, m % CHUNKS
                pe.wait_ge(max_read, done(u * SLOTS + (m - 1 if m > 1 else 0)))
                pe.matmul(pmax[m % 2][:], qst[0:SUMS, b, t * P:(t + 1) * P],
                          kst[0:SUMS, par, j * BANK:(j + 1) * BANK], start=True,
                          stop=True).then_inc(max_mm, 1)

            def transpose_shift(u):
                pe.wait_ge(packed, done(u + 1))
                pe.wait_ge(max_read, done(u * SLOTS + MAXES - 1))
                pe.transpose(pmax[0][0:2 * QT, 0:P], mneg[:], ident[:]).then_inc(max_mm, 1)

            def scores(u, kt, par, b):
                pe.wait_ge(exped, done(u * KT + kt - 1))
                for half in range(2):
                    at = slice(half * BANK, (half + 1) * BANK)
                    mm = pe.matmul(pscore[kt % 2][:, at], kst[0:FULL, par, kt * P:(kt + 1) * P],
                                   qst[0:FULL, b, at], start=True, stop=True)
                mm.then_inc(scored, 1)

            def times_v(u, head, par, c, pair):
                if pair == 0:
                    pe.wait_ge(out_read, done(u))
                    if c == 0:
                        pe.wait_ge(v_in, done(head + 1))
                pe.wait_ge(exped, done(u * KT + 2 * pair + 2))
                for half in range(2):
                    for odd in range(2):
                        kt = 2 * pair + odd
                        row = (half * 2 + odd) * HD
                        mm = pe.matmul(pout[row:row + HD, :], vst[:, par, kt, :],
                                       prob[:, kt % PBUF, half * BANK:(half + 1) * BANK],
                                       start=(pair == 0), stop=(pair == PAIRS - 1))
                mm.then_inc(times_v_done, 1)

            def denominators(u, o):
                if o == 0:
                    pe.wait_ge(den_read, done(u))
                pe.wait_ge(pool_added, done((u * OCTS + o + 1) * ADDS))
                for half in range(2):
                    for s in range(2):
                        row = (half * 2 + s) * HD
                        mm = pe.matmul(pden[row:row + 1, :], ones[:],
                                       sums[:, o % 2, s, half * BANK:(half + 1) * BANK],
                                       start=(o == 0), stop=(o == OCTS - 1))
                mm.then_inc(den_done, 1)

            pe.wait_ge(q_in[0], done(48))
            pe.wait_ge(k_in[0], done(48))
            for m in range(MAXES):
                max_product(0, m, 0, 0)
            transpose_shift(0)

            def turn(i, first, final):
                for u, head, par, c in units(i):
                    npar, nb = (par if c < UNITS - 1 else 1 - par), (c + 1) % 2
                    ahead = not (final and par * UNITS + c == TURN - 1)
                    behind = not (first and par == c == 0)
                    if ahead:
                        nxt = par * UNITS + c + 1
                        pe.wait_ge(q_in[nb], done((i * (TURN // 2) + nxt // 2 + 1) * 48))
                        if c == UNITS - 1:
                            pe.wait_ge(k_in[npar], done((i + (1 if npar == 0 else 0) + 1) * 48))
                    pe.wait_ge(shift_in, done((u + 1) * 32))
                    for pair in range(PAIRS):
                        for odd in range(2):
                            scores(u, 2 * pair + odd, par, c % 2)
                            if ahead:
                                for m in slots(pair, odd):
                                    max_product(u + 1, m, npar, nb)
                        if pair:
                            times_v(u, head, par, c, pair - 1)
                        elif behind:
                            times_v(u - 1, head, par if c else 1 - par, (c - 1) % UNITS, PAIRS - 1)
                        if ahead:
                            for m in slots(pair, 2):
                                max_product(u + 1, m, npar, nb)
                            if pair == PAIRS - 2:
                                transpose_shift(u + 1)
                        if pair % (OCT // 2) == OCT // 2 - 1:
                            o = pair // (OCT // 2)
                            if o:
                                denominators(u, o - 1)
                            elif behind:
                                denominators(u - 1, OCTS - 1)

            turn(0, True, False)
            with pe.Fori(1, TURNS - 1) as i:
                turn(i, False, False)
            turn(TURNS - 1, False, True)
            times_v(ALL - 1, HEADS - 1, 1, UNITS - 1, PAIRS - 1)
            denominators(ALL - 1, OCTS - 1)

        @block.scalar
        def _(act):
            def read_out(u):
                act.wait_ge(times_v_done, done((u + 1) * PAIRS))
                act.wait_ge(out_stored, done(u * 32))
                act.activation(outn[:], pout[:], ACT.Copy).then_inc(out_read, 1)

            def read_den(u):
                act.wait_ge(den_done, done((u + 1) * OCTS))
                act.wait_ge(den_stored, done(u * 32))
                for row in range(0, P, HD):
                    last = act.activation(outd[row:row + 1, :], pden[row:row + 1, :], ACT.Copy)
                last.then_inc(den_read, 1)

            def unit(u, behind):
                for kt in range(KT):
                    if kt % 2 == 0:
                        act.wait_ge(times_v_done, done(u * PAIRS + kt // 2 - PBUF // 2 + 1))
                    if kt % OCT == 0:
                        act.wait_ge(pool_added, done((u * OCTS + kt // OCT - 1) * ADDS))
                    act.wait_ge(scored, done(u * KT + kt + 1))
                    act.activation(prob[:, kt % PBUF, :], pscore[kt % 2][:], ACT.Exp,
                                   scale=SCALE).then_inc(exped, 1)
                    if behind and kt == 2:
                        read_out(u - 1)
                    if behind and kt == OCT + 2:
                        read_den(u - 1)

            unit(0, False)
            with act.Fori(1, ALL) as u:
                unit(u, True)
            read_out(ALL - 1)
            read_den(ALL - 1)

        @block.vector
        def _(dve):
            def small(u, n):
                dve.wait_ge(mlink, done(u * 2 + n))

            def read_max(u, m):
                t, j = m // CHUNKS, m % CHUNKS
                dve.wait_ge(max_mm, done(u * SLOTS + m + 1))
                dve.tensor_reduce(mx[:, t, j:j + 1], pmax[m % 2][:], AX.X, ALU.max).then_inc(max_read, 1)

            def pack_shift(u):
                dve.wait_ge(max_read, done(u * SLOTS + MAXES))
                dve.tensor_reduce(mtop[:], mx[:], AX.X, ALU.max).then_inc(mlink, 1)
                small(u, 1)
                dve.wait_ge(max_mm, done(u * SLOTS))
                dve.tensor_scalar(mneg[:, 0:QT].bitcast(F32R), mtop[:], -1.0, None, ALU.mult).then_inc(mlink, 1)
                small(u, 2)
                dve.scalar_tensor_tensor(mneg[:, QT:2 * QT], mtop[:], -1.0, mneg[:, 0:QT], ALU.mult,
                                         ALU.subtract).then_inc(packed, 1)
                dve.wait_ge(max_mm, done(u * SLOTS + SLOTS))
                dve.wait_ge(shift_in, done(u * 32))
                dve.tensor_copy(mrow[:], pmax[0][0:2 * QT, 0:P]).then_inc(max_read, 1)

            def add(g, b):
                dve.wait_ge(den_done, done(g - 1))
                dve.wait_ge(exped, done(g * OCT + 6))
                dve.tensor_tensor(sums[:, b, 1, :], prob[:, b * OCT + 4, :], prob[:, b * OCT + 5, :],
                                  ALU.add).then_inc(dve_added, 1)

            def copy_v(head, par):
                dve.tensor_copy(vst[:, par, :, :], v_tok[:, :, bass.ds(head * HD, HD)]).then_inc(v_in, 1)

            dve.memset(ones[:], 1.0).then_inc(consts, 1)
            for par in range(2):
                dve.memset(kst[SUMS:P, par, :].bitcast(F32), 1.0).then_inc(consts, 1)
            copy_v(0, 0)
            for m in range(MAXES):
                read_max(0, m)
            pack_shift(0)

            def turn(i, final):
                for u, head, par, c in units(i):
                    ahead = not (final and par * UNITS + c == TURN - 1)
                    for pair in range(PAIRS):
                        if ahead:
                            for place in range(3):
                                for m in slots(pair, place):
                                    read_max(u + 1, m)
                            if pair == PAIRS - 3:
                                pack_shift(u + 1)
                        if pair % (OCT // 2) == OCT // 2 - 1:
                            o = pair // (OCT // 2)
                            add(u * OCTS + o, o % 2)
                        if c == 1 and pair == 1 and not (final and par == HEADS_PER_TURN - 1):
                            dve.wait_ge(times_v_done, done(head * UNITS * PAIRS))
                            copy_v(head + 1, 1 - par)

            with dve.Fori(0, TURNS - 1) as i:
                turn(i, False)
            turn(TURNS - 1, True)


def stage_output(nc, x, chan_o, woT, scr, x1):
    R2 = 0.5 ** 0.5
    with ExitStack() as ctx:
        def sb(name, shape, dt=F32):
            return ctx.enter_context(nc.sbuf_tensor(name, shape, dt))

        def sem(name):
            return ctx.enter_context(nc.semaphore(name))

        w = sb("c_w", [P, KC, C])
        bo = sb("c_bo", [P, KC])
        bor = sb("c_bor", [P, KC])
        att = sb("c_att", [P, 2, KC, BANK])
        odd = sb("c_odd", [P, 2, KC, BANK])
        rden = sb("c_rden", [P, 2, KC, BANK])
        dens = sb("c_dens", [P, 3, HEADS * N // P])
        ps = [ctx.enter_context(nc.psum_tensor(f"c_ps{i}", [P, BANK], F32)) for i in range(8)]
        w_in = sem("c_w_in")
        x_in = sem("c_x_in")
        att_in = [sem(f"c_att_in{i}") for i in range(2)]
        den_in = sem("c_den_in")
        den_sum = sem("c_den_sum")
        inverted = sem("c_inverted")
        inv_out = sem("c_inv_out")
        joined = sem("c_joined")
        divided = sem("c_divided")
        scaled = sem("c_scaled")
        mm_done = sem("c_mm_done")
        added = sem("c_added")
        block = ctx.enter_context(nc.Block())

        @block.sync
        def _(sp):
            for s in (*att_in, mm_done, added, joined, divided):
                sp.sem_inc(s, CREDIT)
            for s in range(2):
                sp.dma_start(dens[:, s, :], scr.att_den[:, s, :].rearrange(
                    "h (a n) -> h a n", n=HEADS * N // P)).then_inc(den_in, 16)
            sp.dma_start(w[:], woT.rearrange("(k p) o -> p k o", p=P)).then_inc(w_in, 16)
            sp.dma_start(bo[:], chan_o).then_inc(w_in, 16)
            sp.wait_ge(inverted, 1)
            sp.dma_start(scr.att_rden.rearrange("h (a n) -> h a n", n=HEADS * N // P),
                         dens[:, 2, :]).then_inc(inv_out, 16)
            sp.wait_ge(inv_out, 16)
            with sp.Fori(0, CHUNKS // 2) as i:
                for b in range(2):
                    sp.wait_ge(mm_done, done((i * 2 + b) * KC - KC))
                    at = bass.ds((i * 2 + b) * BANK, BANK)
                    for k in range(KC):
                        hs = slice(k * P // HD, (k + 1) * P // HD)
                        sp.dma_start(att[:, b, k, :], scr.att[hs, 0, :, at]).then_inc(att_in[b], 16)
                        sp.dma_start(odd[:, b, k, :], scr.att[hs, 1, :, at]).then_inc(att_in[b], 16)
                        sp.dma_start(rden[:, b, k, :], scr.att_rden[hs, at].unsqueeze(1)
                                     .to_broadcast([P // HD, HD, BANK])).then_inc(att_in[b], 16)

        @block.gpsimd
        def _(pool):
            for k in range(KC):
                pool.dma_start(x1[:, k, :], x[k * P:(k + 1) * P, :]).then_inc(x_in, 16)

        @block.tensor
        def _(pe):
            pe.wait_ge(w_in, 32)
            with pe.Fori(0, CHUNKS // 2) as i:
                for b in range(2):
                    n = i * 2 + b
                    pe.wait_ge(divided, done(n + 1))
                    for t in range(KC):
                        pe.wait_ge(added, done(n * KC + t + 1 - 8))
                        for k in range(KC):
                            mm = pe.matmul(ps[b * KC + t][:], w[:, k, t * P:(t + 1) * P], att[:, b, k, :],
                                           start=(k == 0), stop=(k == KC - 1))
                        mm.then_inc(mm_done, 1)

        @block.scalar
        def _(act):
            act.wait_ge(w_in, 32)
            act.mul(bor[:], bo[:], R2).then_inc(scaled, 1)
            act.wait_ge(scaled, 1)
            act.wait_ge(x_in, 16 * KC)
            for k in range(KC):
                act.activation(x1[:, k, :], x1[:, k, :], ACT.Identity, bias=bor[:, k:k + 1],
                               scale=R2).then_inc(scaled, 1)

        @block.vector
        def _(dve):
            dve.wait_ge(den_in, 32)
            dve.tensor_tensor(dens[:, 0, :], dens[:, 0, :], dens[:, 1, :], ALU.add).then_inc(den_sum, 1)
            dve.wait_ge(den_sum, 1)
            dve.reciprocal(dens[:, 2, :], dens[:, 0, :]).then_inc(inverted, 1)

            def divide(n, turn, b):
                dve.wait_ge(att_in[b], done((turn + 1) * 16 * 3 * KC))
                dve.tensor_tensor(att[:, b, :, :], att[:, b, :, :], odd[:, b, :, :], ALU.add).then_inc(joined, 1)
                dve.wait_ge(joined, done(n + 1))
                dve.tensor_tensor(att[:, b, :, :], att[:, b, :, :], rden[:, b, :, :],
                                  ALU.mult).then_inc(divided, 1)

            divide(0, 0, 0)
            dve.wait_ge(scaled, 1 + KC)

            def pair(i, final):
                for b in range(2):
                    n = i * 2 + b
                    if not (final and b == 1):
                        divide(n + 1, i + b, 1 - b)
                    for t in range(KC):
                        dve.wait_ge(mm_done, done(n * KC + t + 1))
                        at = x1[:, t, bass.ds(n * BANK, BANK)]
                        dve.scalar_tensor_tensor(at, ps[b * KC + t][:], R2, at, ALU.mult,
                                                 ALU.add).then_inc(added, 1)

            with dve.Fori(0, CHUNKS // 2 - 1) as i:
                pair(i, False)
            pair(CHUNKS // 2 - 1, True)


GH = 8
ROLES = 3
GROUPS = C // P
TAPS = 5
PAD = IMG + TAPS - 1
ROWS = BANK // IMG
HPG = P // GH
EPS_ATT = 1e-15


def stage_linear(nc, w_all, dw_all, pw_all, mask_d, heads_d, ident_d, scr, x1):
    DVE_CHUNKS = 6
    UNROLL = 2 * ROLES
    TURNS = GROUPS * ROLES // UNROLL
    RING = 3
    K, V, Q = range(ROLES)

    def order():
        out = []
        late = lambda t: [(t, 1, n) for n in range(DVE_CHUNKS)]
        for t in range(UNROLL):
            out += [(t, 0, n) for n in range(CHUNKS)]
            if t:
                out += late(t - 1)
            out += [(t, 1, n) for n in range(DVE_CHUNKS, CHUNKS)]
        return out + late(UNROLL - 1)

    PIECES = order()
    NP = len(PIECES)
    at = {piece: p for p, piece in enumerate(PIECES)}
    V_PIECES = [p for p in range(NP) if PIECES[p][0] % ROLES == V]
    last_piece = {(t, part): max(p for p, (a, b, _) in enumerate(PIECES) if (a, b) == (t, part))
                  for t in range(UNROLL) for part in range(2)}
    first_piece = {(t, part): min(p for p, (a, b, _) in enumerate(PIECES) if (a, b) == (t, part))
                   for t in range(UNROLL) for part in range(2)}

    with ExitStack() as ctx:
        def sb(name, shape, dt=F32):
            return ctx.enter_context(nc.sbuf_tensor(name, shape, dt))

        def pb(name):
            return ctx.enter_context(nc.psum_tensor(name, [P, BANK], F32))

        def sem(name):
            return ctx.enter_context(nc.semaphore(name))

        w = sb("d_w", [P, 2, KC, P])
        dw = sb("d_dw", [P, 2, TAPS * TAPS])
        pw = sb("d_pw", [P, 2, P])
        bd = sb("d_bd", [P, 2, P])
        wtap = sb("d_wtap", [P, TAPS * TAPS, P])
        ypad = sb("d_ypad", [P, 2, PAD, PAD])
        dsum = sb("d_dsum", [P, 2, DVE_CHUNKS * BANK])
        piece = sb("d_piece", [P, RING, BANK])
        tk = sb("d_tk", [P, 2, N // P, P])
        tv = sb("d_tv", [P, 2, 4, P + 1])
        vks = sb("d_vks", [P, P + 1])
        num_w = sb("d_num_w", [P, 2, P])
        den_w = sb("d_den_w", [P, 2, HPG])
        num = sb("d_num", [P, RING, BANK])
        den = sb("d_den", [HPG, RING, BANK])
        mask = sb("d_mask", [P, P])
        hmask = sb("d_hmask", [P, HPG])
        ident = sb("d_ident", [P, P])
        pmain = [pb(f"d_pmain{i}") for i in range(RING)]
        ptr = [pb(f"d_ptr{i}") for i in range(2)]
        pnum, pden, pvk = pb("d_pnum"), pb("d_pden"), pb("d_pvk")

        consts = sem("d_consts")
        zeroed = sem("d_zeroed")
        loaded = [sem(f"d_loaded{i}") for i in range(2)]
        built = sem("d_built")
        bd_made = sem("d_bd_made")
        main_done = sem("d_main_done")
        main_read = sem("d_main_read")
        post_done = sem("d_post_done")
        post_read = sem("d_post_read")
        vk_done = sem("d_vk_done")
        vk_read = sem("d_vk_read")
        vk_used = sem("d_vk_used")
        dlink = sem("d_dlink")
        stored = [sem(f"d_stored{i}") for i in range(RING)]
        TAPN = TAPS * TAPS

        block = ctx.enter_context(nc.Block())

        @block.sync
        def _(sp):
            for s in (*loaded, built, bd_made, main_done, main_read, post_done, post_read, vk_done,
                      vk_read, vk_used, dlink, *stored):
                sp.sem_inc(s, CREDIT)
            for dst, src in ((mask, mask_d), (hmask, heads_d), (ident, ident_d)):
                sp.dma_start(dst[:], src).then_inc(consts, 16)

            def load(i, t):
                tile, b = i * UNROLL + t, t % 2
                sp.wait_ge(dlink, done((i * UNROLL + t - 1) * TAPN))
                sp.wait_ge(built, done(i * UNROLL + t - 1))
                sp.dma_start(w[:, b, :, :], w_all[tile].rearrange("(k p) o -> p k o", p=P)).then_inc(loaded[b], 16)
                sp.dma_start(dw[:, b, :], dw_all[tile]).then_inc(loaded[b], 16)
                sp.dma_start(pw[:, b, :], pw_all[tile]).then_inc(loaded[b], 16)

            for dst, src in ((w[:, 0, :, :], w_all[0].rearrange("(k p) o -> p k o", p=P)),
                             (dw[:, 0, :], dw_all[0]), (pw[:, 0, :], pw_all[0])):
                sp.dma_start(dst, src).then_inc(loaded[0], 16)

            def turn(i, final):
                for p, (t, part, n) in enumerate(PIECES):
                    if t % ROLES == Q:
                        group = i * 2 + t // ROLES
                        sp.wait_ge(post_read, done(i * NP + p + 1))
                        sp.dma_start(scr.num[part, group, :, n * BANK:(n + 1) * BANK],
                                     num[:, p % RING, :]).then_inc(stored[p % RING], 16)
                        sp.dma_start(scr.den[part, group, :, n * BANK:(n + 1) * BANK],
                                     den[:, p % RING, :]).then_inc(stored[p % RING], 16)
                    if part == 0 and n == CHUNKS - 1 and not (final and t == UNROLL - 1):
                        load(i, t + 1)

            with sp.Fori(0, TURNS - 1) as i:
                turn(i, False)
            turn(TURNS - 1, True)
            for r in range(RING):
                mine = sum(t % ROLES == Q and p % RING == r for p, (t, _, _) in enumerate(PIECES))
                sp.wait_ge(stored[r], done(TURNS * mine * 32))

        @block.gpsimd
        def _(pool):
            pool.wait_ge(consts, 48)

            def build(i, t):
                b = t % 2
                pool.wait_ge(loaded[b], done((i * (UNROLL // 2) + t // 2 + 1) * 48))
                if t >= 2:
                    pool.wait_ge(main_done, done(i * NP + last_piece[t - 2, 1] + 1))
                else:
                    pool.wait_ge(main_done, done(i * NP))
                tile = i * UNROLL + t
                pool.tensor_tensor(bd[:, b, :], pw[:, b, :], mask[:], ALU.mult).then_inc(bd_made, 1)
                pool.wait_ge(bd_made, done(tile + 1))
                pool.wait_ge(main_done, done(i * NP + (at[t - 1, 1, CHUNKS - 1] + 1 if t else 0)))
                pool.tensor_tensor(wtap[:, 0, :], bd[:, b, :], dw[:, b, 0:1].to_broadcast([P, P]), ALU.mult)
                for tap in range(1, TAPN):
                    last = pool.tensor_scalar(wtap[:, tap, :], bd[:, b, :], dw[:, b, tap:tap + 1],
                                              None, ALU.mult)
                last.then_inc(built, 1)

            def blocks(i, g, part):
                count = (i * 2 + g) * 2 + part
                pool.wait_ge(vk_read, done(count + 1))
                t = g * ROLES + Q
                if g:
                    pool.wait_ge(post_done, done(i * NP + last_piece[t - ROLES, part] + 1))
                else:
                    pool.wait_ge(post_done, done(i * NP))
                pool.tensor_tensor(num_w[:, part, :], vks[:, 0:P], mask[:], ALU.mult)
                pool.tensor_scalar(den_w[:, part, :], hmask[:], vks[:, P:P + 1], None,
                                   ALU.mult).then_inc(vk_used, 1)

            with pool.Fori(0, TURNS) as i:
                for g in range(2):
                    build(i, g * ROLES + K)
                    build(i, g * ROLES + V)
                    blocks(i, g, 0)
                    build(i, g * ROLES + Q)
                    blocks(i, g, 1)

        @block.tensor
        def _(pe):
            pe.wait_ge(consts, 48)
            pe.wait_ge(zeroed, 4)

            def main(i, p):
                t, part, n = PIECES[p]
                b = t % 2
                tile = i * UNROLL + t
                pe.wait_ge(main_read, done(i * NP + p + 1 - RING))
                out = pmain[p % RING][:]
                if part == 0:
                    if n == 0:
                        pe.wait_ge(loaded[b], done((i * (UNROLL // 2) + t // 2 + 1) * 48))
                    for k in range(KC):
                        mm = pe.matmul(out, w[:, b, k, :], x1[:, k, n * BANK:(n + 1) * BANK],
                                       start=(k == 0), stop=(k == KC - 1))
                elif n >= DVE_CHUNKS:
                    if n == DVE_CHUNKS:
                        pe.wait_ge(built, done(tile + 1))
                        pe.wait_ge(main_read, done(i * NP + last_piece[t, 0] + 1))
                    for tap in range(TAPN):
                        dy, dx = tap // TAPS, tap % TAPS
                        mm = pe.matmul(out.rearrange("p (r c) -> p r c", c=IMG), wtap[:, tap, :],
                                       ypad[:, b, n * ROWS + dy:(n + 1) * ROWS + dy, dx:dx + IMG],
                                       start=(tap == 0), stop=(tap == TAPN - 1))
                else:
                    if n == 0:
                        pe.wait_ge(dlink, done((tile + 1) * TAPN))
                        pe.wait_ge(built, done(tile + 1))
                    mm = pe.matmul(out, bd[:, b, :], dsum[:, b, n * BANK:(n + 1) * BANK],
                                   start=True, stop=True)
                mm.then_inc(main_done, 1)

            def post(i, p):
                t, part, n = PIECES[p]
                role, group = t % ROLES, i * 2 + t // ROLES
                pe.wait_ge(main_read, done(i * NP + p + 1))
                if role == Q:
                    if p == first_piece[t, part]:
                        pe.wait_ge(vk_used, done(group * 2 + part + 1))
                    pe.wait_ge(post_read, done(i * NP + p))
                    pe.matmul(pnum[:], num_w[:, part, :], piece[:, p % RING, :], start=True, stop=True)
                    pe.matmul(pden[0:HPG, :], den_w[:, part, :], piece[:, p % RING, :], start=True,
                              stop=True).then_inc(post_done, 1)
                else:
                    pe.wait_ge(post_read, done(i * NP + p - 1))
                    for s in range(4):
                        tr = pe.transpose(ptr[p % 2][:, s * P:(s + 1) * P],
                                          piece[:, p % RING, s * P:(s + 1) * P], ident[:])
                    tr.then_inc(post_done, 1)

            def times_k(i, p):
                t, part, n = PIECES[p]
                if t % ROLES != V:
                    return
                pe.wait_ge(post_read, done(i * NP + p + 1))
                first, last = p == first_piece[t, part], p == last_piece[t, part]
                if first:
                    pe.wait_ge(vk_read, done((i * 2 + t // ROLES) * 2 + part))
                for s in range(4):
                    mm = pe.matmul(pvk[:, 0:P + 1], tk[:, part, n * 4 + s, :], tv[:, V_PIECES.index(p) % 2, s, :],
                                   start=(first and s == 0), stop=(last and s == 3))
                mm.then_inc(vk_done, 1)

            with pe.Fori(0, TURNS) as i:
                for p in range(NP + 2):
                    if p < NP:
                        main(i, p)
                    if p >= 2:
                        times_k(i, p - 2)
                    if 1 <= p <= NP:
                        post(i, p - 1)

        @block.scalar
        def _(act):
            act.wait_ge(zeroed, 4)

            def read_main(i, p):
                t, part, n = PIECES[p]
                b, role = t % 2, t % ROLES
                tile = i * UNROLL + t
                act.wait_ge(main_done, done(i * NP + p + 1))
                src = pmain[p % RING][:]
                if part == 0:
                    if n == 0:
                        if t:
                            act.wait_ge(dlink, done((tile - 1) * TAPN))
                        act.wait_ge(post_done, done(i * NP + (at[t - 2, 1, CHUNKS - 1] + 1 if t >= 2 else 0)))
                    act.activation(ypad[:, b, 2 + n * ROWS:2 + (n + 1) * ROWS, 2:2 + IMG],
                                   src.rearrange("p (r c) -> p r c", c=IMG), ACT.Copy)
                act.wait_ge(post_done, done(i * NP + p + 1 - RING))
                act.activation(piece[:, p % RING, :], src,
                               ACT.Copy if role == V else ACT.Relu).then_inc(main_read, 1)

            def read_post(i, p):
                t, part, n = PIECES[p]
                role, group = t % ROLES, i * 2 + t // ROLES
                act.wait_ge(post_done, done(i * NP + p + 1))
                if role == K:
                    if p == first_piece[t, part]:
                        act.wait_ge(vk_read, done((group - 1) * 2 + part + 1))
                    act.activation(tk[:, part, n * 4:(n + 1) * 4, :],
                                   ptr[p % 2][:].rearrange("p (s c) -> p s c", c=P),
                                   ACT.Copy).then_inc(post_read, 1)
                elif role == V:
                    k = V_PIECES.index(p)
                    act.wait_ge(vk_done, done(i * len(V_PIECES) + k - 1))
                    act.activation(tv[:, k % 2, :, 0:P], ptr[p % 2][:].rearrange("p (s c) -> p s c", c=P),
                                   ACT.Copy).then_inc(post_read, 1)
                else:
                    r = p % RING
                    mine = [x for x in range(NP) if PIECES[x][0] % ROLES == Q and x % RING == r]
                    act.wait_ge(stored[r], done((i * len(mine) + mine.index(p)) * 32))
                    act.activation(num[:, r, :], pnum[:], ACT.Copy)
                    act.activation(den[:, r, :], pden[0:HPG, :], ACT.Copy, bias=EPS_ATT).then_inc(post_read, 1)

            def read_vk(i, p):
                t, part, _ = PIECES[p]
                if t % ROLES == V and p == last_piece[t, part]:
                    count = (i * 2 + t // ROLES) * 2 + part
                    act.wait_ge(vk_done, done(i * len(V_PIECES) + V_PIECES.index(p) + 1))
                    act.wait_ge(vk_used, done(count))
                    act.activation(vks[:], pvk[:, 0:P + 1], ACT.Copy).then_inc(vk_read, 1)

            with act.Fori(0, TURNS) as i:
                for p in range(NP + 2):
                    if p < NP:
                        read_main(i, p)
                    if p >= 2:
                        read_vk(i, p - 2)
                    if 1 <= p <= NP:
                        read_post(i, p - 1)

        @block.vector
        def _(dve):
            for b in range(2):
                dve.memset(ypad[:, b, :, :], 0.0).then_inc(zeroed, 1)
                dve.memset(tv[:, b, :, P:P + 1], 1.0).then_inc(zeroed, 1)
            with dve.Fori(0, TURNS) as i:
                for t in range(UNROLL):
                    b = t % 2
                    tile = i * UNROLL + t
                    dve.wait_ge(loaded[b], done((i * (UNROLL // 2) + t // 2 + 1) * 48))
                    dve.wait_ge(main_read, done(i * NP + last_piece[t, 0] + 1))
                    dve.wait_ge(main_done, done(i * NP + (at[t - 2, 1, DVE_CHUNKS - 1] + 1 if t >= 2 else 0)))
                    acc = dsum[:, b, :].rearrange("p (r c) -> p r c", c=IMG)
                    for tap in range(TAPN):
                        dy, dx = tap // TAPS, tap % TAPS
                        src = ypad[:, b, dy:dy + DVE_CHUNKS * ROWS, dx:dx + IMG]
                        if tap == 0:
                            add = dve.tensor_scalar(acc, src, dw[:, b, tap:tap + 1], None, ALU.mult)
                        else:
                            dve.wait_ge(dlink, done(tile * TAPN + tap))
                            add = dve.scalar_tensor_tensor(acc, src, dw[:, b, tap:tap + 1], acc,
                                                           ALU.mult, ALU.add)
                        add.then_inc(dlink, 1)


def stage_project(nc, wprojT, chan_bn, scr, x1, out):
    BN_EPS = 1e-5
    MS = 2 * GROUPS
    HALF = N // 2
    with ExitStack() as ctx:
        def sb(name, shape, dt=F32):
            return ctx.enter_context(nc.sbuf_tensor(name, shape, dt))

        def sem(name):
            return ctx.enter_context(nc.semaphore(name))

        w = sb("f_w", [P, MS, C])
        par = sb("f_par", [P, KC, 2])
        num = sb("f_num", [P, 2, MS, BANK])
        rden = sb("f_rden", [P, 2, GROUPS, BANK])
        proj = sb("f_proj", [P, KC, N])
        stats = sb("f_stats", [P, KC, CHUNKS, 6])
        mv = sb("f_mv", [P, KC, 2])
        coef = sb("f_coef", [P, 2, KC])
        var = sb("f_var", [P, KC])
        sd = sb("f_sd", [P, KC])
        rstd = sb("f_rstd", [P, KC])
        tmp = sb("f_tmp", [P, KC])
        ps = [ctx.enter_context(nc.psum_tensor(f"f_ps{i}", [P, BANK], F32)) for i in range(8)]

        den_in = sem("f_den_in")
        inverted = sem("f_inverted")
        inv_out = sem("f_inv_out")
        w_in = sem("f_w_in")
        num_in = [sem(f"f_num_in{i}") for i in range(2)]
        rden_in = [sem(f"f_rden_in{i}") for i in range(2)]
        divided = sem("f_divided")
        mm_done = sem("f_mm_done")
        copied = sem("f_copied")
        measured = sem("f_measured")
        link_s = sem("f_link")
        var_ready = sem("f_var_ready")
        root = sem("f_root")
        coef_ready = sem("f_coef_ready")
        scaled = sem("f_scaled")
        summed = sem("f_summed")
        stored = sem("f_stored")
        block = ctx.enter_context(nc.Block())

        @block.sync
        def _(sp):
            for s in (*num_in, *rden_in, divided, mm_done, copied, measured):
                sp.sem_inc(s, CREDIT)
            sp.dma_start(proj[:, 0, :], scr.den.rearrange("a g h n -> (a g h) n")).then_inc(den_in, 16)
            sp.dma_start(w[:], wprojT.rearrange("(m p) o -> p m o", p=P)).then_inc(w_in, 16)
            sp.dma_start(par[:], chan_bn).then_inc(w_in, 16)
            sp.wait_ge(inverted, 1)
            sp.dma_start(scr.rden, proj[:, 1, :]).then_inc(inv_out, 16)
            sp.wait_ge(inv_out, 16)
            with sp.Fori(0, CHUNKS // 2) as i:
                for b in range(2):
                    n = i * 2 + b
                    at = bass.ds(n * BANK, BANK)
                    sp.wait_ge(mm_done, done(n * KC - KC))
                    sp.dma_start(num[:, b, :, :], scr.num.rearrange("a g p n -> p (a g) n")[
                        :, :, at]).then_inc(num_in[b], 16)
                    for part in range(2):
                        sp.wait_ge(divided, done(n * 2 + part - 1))
                        for g in range(GROUPS):
                            row = (part * GROUPS + g) * HPG
                            sp.dma_start(rden[:, part, g, :], scr.rden[row:row + HPG, at].unsqueeze(1)
                                         .to_broadcast([HPG, GH, BANK])).then_inc(rden_in[part], 16)
            for t in range(KC):
                for h in range(2):
                    sp.wait_ge(summed, t * 2 + h + 1)
                    sp.dma_start(out[t * P:(t + 1) * P, h * HALF:(h + 1) * HALF],
                                 proj[:, t, h * HALF:(h + 1) * HALF]).then_inc(stored, 16)
            sp.wait_ge(stored, KC * 2 * 16)

        @block.tensor
        def _(pe):
            pe.wait_ge(w_in, 32)
            with pe.Fori(0, CHUNKS // 2) as i:
                for b in range(2):
                    n = i * 2 + b
                    for t in range(KC):
                        if t == 0:
                            pe.wait_ge(divided, done(n * 2 + 2))
                        pe.wait_ge(copied, done(n * KC + t + 1 - 8))
                        for m in range(MS):
                            mm = pe.matmul(ps[b * KC + t][:], w[:, m, t * P:(t + 1) * P], num[:, b, m, :],
                                           start=(m == 0), stop=(m == MS - 1))
                        mm.then_inc(mm_done, 1)

        @block.scalar
        def _(act):
            act.wait_ge(inv_out, 16)
            with act.Fori(0, CHUNKS // 2) as i:
                for b in range(2):
                    n = i * 2 + b
                    for t in range(KC):
                        act.wait_ge(mm_done, done(n * KC + t + 1))
                        act.activation(proj[:, t, bass.ds(n * BANK, BANK)], ps[b * KC + t][:],
                                       ACT.Copy).then_inc(copied, 1)
            act.wait_ge(var_ready, 1)
            act.activation(sd[:], var[:], ACT.Sqrt).then_inc(root, 1)
            act.wait_ge(coef_ready, 1)
            for t in range(KC):
                for h in range(2):
                    at = proj[:, t, h * HALF:(h + 1) * HALF]
                    act.activation(at, at, ACT.Identity, bias=coef[:, 1, t:t + 1],
                                   scale=coef[:, 0, t:t + 1]).then_inc(scaled, 1)

        @block.vector
        def _(dve):
            links = 0

            def link(ins):
                nonlocal links
                links += 1
                ins.then_inc(link_s, 1)
                dve.wait_ge(link_s, links)

            dve.wait_ge(den_in, 16)
            dve.reciprocal(proj[:, 1, :], proj[:, 0, :]).then_inc(inverted, 1)

            def divide(n, b):
                for part in range(2):
                    if part == 0:
                        dve.wait_ge(num_in[b], done(16 * (n // 2 + 1)))
                    dve.wait_ge(rden_in[part], done(64 * (n + 1)))
                    at = num[:, b, part * GROUPS:(part + 1) * GROUPS, :]
                    dve.tensor_tensor(at, at, rden[:, part, :, :], ALU.mult).then_inc(divided, 1)

            def measure(n):
                for t in range(KC):
                    dve.wait_ge(copied, done(n * KC + t + 1))
                    dve.bn_stats(stats[:, t, n, :], proj[:, t, n * BANK:(n + 1) * BANK]).then_inc(measured, 1)

            divide(0, 0)
            for n in range(CHUNKS):
                if n + 1 < CHUNKS:
                    divide(n + 1, (n + 1) % 2)
                measure(n)
            dve.wait_ge(w_in, 32)
            dve.wait_ge(measured, done(KC * CHUNKS))
            for t in range(KC):
                last = dve.bn_aggr(mv[:, t, :], stats[:, t, :, :].rearrange("p j s -> p (j s)"))
            link(last)
            dve.tensor_scalar(var[:], mv[:, :, 1], BN_EPS, None, ALU.add).then_inc(var_ready, 1)
            dve.wait_ge(root, 1)
            link(dve.reciprocal(rstd[:], sd[:]))
            link(dve.tensor_tensor(tmp[:], rstd[:], rstd[:], ALU.mult))
            link(dve.tensor_tensor(tmp[:], tmp[:], var[:], ALU.mult))
            link(dve.tensor_scalar(tmp[:], tmp[:], -0.5, 1.5, ALU.mult, ALU.add))
            link(dve.tensor_tensor(rstd[:], rstd[:], tmp[:], ALU.mult))
            link(dve.tensor_tensor(coef[:, 0, :], rstd[:], par[:, :, 0], ALU.mult))
            link(dve.tensor_tensor(tmp[:], mv[:, :, 0], coef[:, 0, :], ALU.mult))
            dve.tensor_tensor(coef[:, 1, :], par[:, :, 1], tmp[:], ALU.subtract).then_inc(coef_ready, 1)
            for t in range(KC):
                for h in range(2):
                    dve.wait_ge(scaled, t * 2 + h + 1)
                    at = slice(h * HALF, (h + 1) * HALF)
                    dve.tensor_tensor(proj[:, t, at], proj[:, t, at], x1[:, t, at], ALU.add).then_inc(summed, 1)


def conv_seq(nc, x, chan, wqT, wkT, wvT, bv, bo, woT, w_all, dw_all, pw_all, wprojT, chan_bn,
             group_mean, mask, hmask, ident, out):
    scr = Scratch(nc)
    with nc.sbuf_tensor("v_tok", [P, N // P, C], F32) as v_tok:
        stage_qkv(nc, x, chan, wqT, wkT, wvT, bv, group_mean, scr, v_tok)
        stage_attention(nc, scr, v_tok, ident)
    with nc.sbuf_tensor("x1", [P, KC, N], F32) as x1:
        stage_output(nc, x, bo, woT, scr, x1)
        stage_linear(nc, w_all, dw_all, pw_all, mask, hmask, ident, scr, x1)
        stage_project(nc, wprojT, chan_bn, scr, x1, out)


def kernel(**inputs):
    import numpy as np
    import concourse.bacc as bacc
    from concourse.bass_utils import run_bass_kernel_spmd as run

    def by_channel(*vectors):
        return np.stack([np.asarray(v).reshape(KC, P) for v in vectors], -1).transpose(1, 0, 2)

    a = {n: np.asarray(v) for n, v in inputs.items()}
    l0 = {n[len("L0_conv_"):]: v for n, v in a.items() if n.startswith("L0_conv_")}
    l1 = {n[len("L1_conv_"):]: v for n, v in a.items() if n.startswith("L1_conv_")}
    roles = [1, 2, 0]
    w_all = l1["w_qkv"].reshape(GROUPS, HPG, ROLES, GH, C)[:, :, roles].transpose(0, 2, 4, 1, 3)
    dw_all = l1["w_dw"].reshape(GROUPS, HPG, ROLES, GH, TAPS * TAPS)[:, :, roles].transpose(0, 2, 1, 3, 4)
    pw = l1["w_pw"].reshape(GROUPS, HPG, ROLES, GH, GH)[:, :, roles].transpose(0, 2, 1, 4, 3)
    pw_all = np.tile(pw.reshape(GROUPS * ROLES, P, GH), (1, 1, HPG))
    eye = np.eye(P, dtype=np.float32)
    arrays = {
        "x": a["x"].reshape(C, N),
        "chan": by_channel(l0["gn_w"], l0["gn_b"], l0["bq"], l0["bk"]),
        "wqT": l0["wq"].T, "wkT": l0["wk"].T, "wvT": l0["wv"].T, "bv": l0["bv"],
        "bo": by_channel(l0["bo"])[:, :, 0],
        "woT": l0["wo"].T,
        "w_all": w_all.reshape(GROUPS * ROLES, C, P),
        "dw_all": dw_all.reshape(GROUPS * ROLES, P, TAPS * TAPS),
        "pw_all": pw_all,
        "wprojT": l1["w_proj"].T,
        "chan_bn": by_channel(l1["bn_gamma"], l1["bn_beta"]),
        "group_mean": np.kron(np.eye(P // GN_GROUP), np.full((GN_GROUP, GN_GROUP), 1.0 / GN_GROUP)).astype(np.float32),
        "mask": np.kron(np.eye(HPG), np.ones((GH, GH))).astype(np.float32),
        "hmask": np.kron(np.eye(HPG), np.ones((GH, 1))).astype(np.float32),
        "ident": eye,
    }
    nc = bacc.Bacc("TRN2", target_bir_lowering=False, num_devices=1)
    args, ins = [], {}
    for name, v in arrays.items():
        v = np.ascontiguousarray(v)
        ins[f"in_{name}"] = v
        args.append(nc.dram_tensor(f"in_{name}", v.shape, mybir.dt.from_np(v.dtype), kind="ExternalInput").ap())
    out = nc.dram_tensor("out_0", (1, C, IMG, IMG), F32, kind="ExternalOutput").ap()
    conv_seq(nc, *args, out.rearrange("b c h w -> (b c) (h w)"))
    r = run(nc, [ins], core_ids=[0])
    return r.results[0]["out_0"]
```

```python
from contextlib import ExitStack

import concourse.bass as bass
from concourse import mybir

F32 = mybir.dt.float32
F32R = mybir.dt.float32r
ALU = mybir.AluOpType
ACT = mybir.ActivationFunctionType
AX = mybir.AxisListType

P = 128
C = 512
IMG = 64
N = IMG * IMG
KC = C // P
BANK = 512
CHUNKS = N // BANK

GN_GROUP = 16
GN_EPS = 1e-6
HEADS = 16
HD = C // HEADS
SCALE = float(HD) ** -0.5

CREDIT = 8


def done(n):
    return n + CREDIT


class Scratch:

    def __init__(self, nc):
        self.qh = nc.dram_tensor("scratch_qh", (C, N), F32, kind="Internal").ap()
        self.ql = nc.dram_tensor("scratch_ql", (C, N), F32, kind="Internal").ap()
        self.kh = nc.dram_tensor("scratch_kh", (C, N), F32, kind="Internal").ap()
        self.kl = nc.dram_tensor("scratch_kl", (C, N), F32, kind="Internal").ap()
        self.num = nc.dram_tensor("scratch_num", (2, GROUPS, P, N), F32, kind="Internal").ap()
        self.den = nc.dram_tensor("scratch_den", (2, GROUPS, HPG, N), F32, kind="Internal").ap()
        self.rden = nc.dram_tensor("scratch_rden", (2 * GROUPS * HPG, N), F32, kind="Internal").ap()
        self.att = nc.dram_tensor("scratch_att", (HEADS, 2, HD, N), F32, kind="Internal").ap()
        self.att_den = nc.dram_tensor("scratch_att_den", (HEADS, 2, N), F32, kind="Internal").ap()
        self.att_rden = nc.dram_tensor("scratch_att_rden", (HEADS, N), F32, kind="Internal").ap()


def stage_qkv(nc, x, chan, wqT, wkT, wvT, bv, group_mean, scr, v_tok):
    with ExitStack() as ctx:
        def sb(name, shape, dt=F32):
            return ctx.enter_context(nc.sbuf_tensor(name, shape, dt))

        def sem(name):
            return ctx.enter_context(nc.semaphore(name))

        xs = sb("a_x", [P, KC, N])
        w = {r: sb(f"a_w{r}", [P, KC, C]) for r in "qkv"}
        par = sb("a_par", [P, KC, 4])
        bv_rows = sb("a_bv_rows", [P, C])
        gmean = sb("a_gmean", [P, P])
        stats = sb("a_stats", [P, KC, CHUNKS, 6])
        mv = sb("a_mv", [P, KC, 2])
        dev = sb("a_dev", [P, KC])
        spread = sb("a_spread", [P, KC])
        mean = sb("a_mean", [P, KC])
        rstd = sb("a_rstd", [P, KC])
        tmp = sb("a_tmp", [P, KC])
        var = sb("a_var", [P, KC])
        sd = sb("a_sd", [P, KC])
        aff = sb("a_aff", [P, 2, 2, KC])
        vn = sb("a_vn", [P, 2, KC, BANK])
        high = sb("a_high", [P, 2, 4, BANK], F32R)
        low = sb("a_low", [P, 2, 4, BANK], F32R)
        ps = [ctx.enter_context(nc.psum_tensor(f"a_ps{i}", [P, BANK], F32)) for i in range(8)]

        x_in = [sem(f"a_x_in{k}") for k in range(KC)]
        par_in = sem("a_par_in")
        w_in = sem("a_w_in")
        stat = sem("a_stat")
        moments = sem("a_moments")
        spread_ready = sem("a_spread_ready")
        gsum = sem("a_gsum")
        var_ready = sem("a_var_ready")
        root = sem("a_root")
        coef = sem("a_coef")
        qn_ready = sem("a_qn_ready")
        vn_ready = sem("a_vn_ready")
        mm_done = sem("a_mm_done")
        high_done = sem("a_high_done")
        low_done = sem("a_low_done")
        v_done = sem("a_v_done")
        stored = [sem(f"a_stored_{r}") for r in "qk"]

        TILES = 12
        block = ctx.enter_context(nc.Block())

        @block.sync
        def _(sp):
            for k in range(KC):
                sp.dma_start(xs[:, k, :], x[k * P:(k + 1) * P, :]).then_inc(x_in[k], 16)
            sp.dma_start(par[:], chan).then_inc(par_in, 16)
            sp.dma_start(gmean[:], group_mean).then_inc(par_in, 16)
            sp.dma_start(bv_rows[:], bv.partition_broadcast(P)).then_inc(par_in, 16)
            for r, src in (("q", wqT), ("k", wkT), ("v", wvT)):
                sp.dma_start(w[r][:], src.rearrange("(k p) o -> p k o", p=P)).then_inc(w_in, 16)
            with sp.Fori(0, CHUNKS // 2) as i:
                for b in range(2):
                    n = i * 2 + b
                    for r, (hi_d, lo_d) in enumerate(((scr.qh, scr.ql), (scr.kh, scr.kl))):
                        sp.wait_ge(low_done, done(n * 8 + 4 * r + 4))
                        for dst, src in ((hi_d, high), (lo_d, low)):
                            sp.dma_start(
                                dst.rearrange("(k p) n -> p k n", p=P)[:, :, bass.ds(n * BANK, BANK)],
                                src[:, r, :, :].bitcast(F32)).then_inc(stored[r], 16)
            for s in stored:
                sp.wait_ge(s, done(CHUNKS * 2 * 16))

        @block.vector
        def _(dve):
            for s in (low_done, v_done):
                dve.sem_inc(s, CREDIT)
            links = 0

            def link(ins):
                nonlocal links
                links += 1
                ins.then_inc(stat, 1)
                dve.wait_ge(stat, links)

            for k in range(KC):
                dve.wait_ge(x_in[k], 16)
                for j in range(CHUNKS):
                    last = dve.bn_stats(stats[:, k, j, :], xs[:, k, j * BANK:(j + 1) * BANK])
            link(last)
            for k in range(KC):
                last = dve.bn_aggr(mv[:, k, :], stats[:, k, :, :].rearrange("p j s -> p (j s)"))
            link(last)
            dve.wait_ge(par_in, 16 * 3)

            def affine(norm):
                dve.sem_inc(moments, 1)
                dve.wait_ge(gsum, 2 * norm + 1)
                link(dve.tensor_copy(mean[:], ps[0][:, 0:KC]))
                link(dve.tensor_tensor(dev[:], mv[:, :, 0], mean[:], ALU.subtract))
                link(dve.tensor_tensor(dev[:], dev[:], dev[:], ALU.mult))
                dve.tensor_tensor(spread[:], dev[:], mv[:, :, 1], ALU.add).then_inc(spread_ready, 1)
                dve.wait_ge(gsum, 2 * norm + 2)
                dve.tensor_scalar(var[:], ps[1][:, 0:KC], GN_EPS, None, ALU.add).then_inc(var_ready, 1)
                dve.wait_ge(root, norm + 1)
                link(dve.reciprocal(rstd[:], sd[:]))
                link(dve.tensor_tensor(tmp[:], rstd[:], rstd[:], ALU.mult))
                link(dve.tensor_tensor(tmp[:], tmp[:], var[:], ALU.mult))
                link(dve.tensor_scalar(tmp[:], tmp[:], -0.5, 1.5, ALU.mult, ALU.add))
                link(dve.tensor_tensor(rstd[:], rstd[:], tmp[:], ALU.mult))
                link(dve.tensor_tensor(aff[:, norm, 0, :], rstd[:], par[:, :, 0], ALU.mult))
                link(dve.tensor_tensor(tmp[:], mean[:], aff[:, norm, 0, :], ALU.mult))
                return dve.tensor_tensor(aff[:, norm, 1, :], par[:, :, 1], tmp[:], ALU.subtract)

            link(affine(0))
            link(dve.tensor_tensor(tmp[:], mv[:, :, 0], aff[:, 0, 0, :], ALU.mult))
            link(dve.tensor_tensor(mv[:, :, 0], tmp[:], aff[:, 0, 1, :], ALU.add))
            link(dve.tensor_tensor(tmp[:], mv[:, :, 1], aff[:, 0, 0, :], ALU.mult))
            link(dve.tensor_tensor(mv[:, :, 1], tmp[:], aff[:, 0, 0, :], ALU.mult))
            link(affine(1))
            dve.sem_inc(coef, 1)
            for at in (slice(0, BANK), slice(BANK, N)):
                for k in range(KC):
                    dve.tensor_scalar(xs[:, k, at], xs[:, k, at], aff[:, 0, 0, k:k + 1],
                                      aff[:, 0, 1, k:k + 1], ALU.mult, ALU.add).then_inc(qn_ready, 1)

            with dve.Fori(0, CHUNKS // 2) as i:
                for b in range(2):
                    n = i * 2 + b
                    for m in range(8):
                        r, t = m // 4, m % 4
                        g = b * TILES + m
                        dve.wait_ge(high_done, done(n * 8 + m + 1))
                        if t == 0:
                            dve.wait_ge(stored[r], done(n * 32))
                        bias = par[:, t, 2 + r:3 + r]
                        dve.scalar_tensor_tensor(low[:, r, t, :], ps[g % 8][:], bias,
                                                 high[:, r, t, :].bitcast(F32), ALU.add,
                                                 ALU.subtract).then_inc(low_done, 1)
                    for t in range(4):
                        g = b * TILES + 8 + t
                        dve.wait_ge(mm_done, done(n * TILES + 8 + t + 1))
                        dve.tensor_tensor(v_tok[:, n * 4 + t, :], ps[g % 8][:], bv_rows[:],
                                          ALU.add).then_inc(v_done, 1)

        @block.scalar
        def _(act):
            act.sem_inc(high_done, CREDIT)
            act.sem_inc(vn_ready, CREDIT)
            for norm in range(2):
                act.wait_ge(var_ready, norm + 1)
                act.activation(sd[:], var[:], ACT.Sqrt).then_inc(root, 1)
            act.wait_ge(coef, 1)
            act.wait_ge(qn_ready, KC)

            def normalise(n, b):
                for k in range(KC):
                    last = act.activation(vn[:, b, k, :], xs[:, k, bass.ds(n * BANK, BANK)], ACT.Identity,
                                          bias=aff[:, 1, 1, k:k + 1], scale=aff[:, 1, 0, k:k + 1])
                last.then_inc(vn_ready, 1)

            def pair(i, final):
                for b in range(2):
                    n = i * 2 + b
                    if not (final and b == 1):
                        act.wait_ge(qn_ready, 2 * KC)
                        act.wait_ge(mm_done, done(n * TILES))
                        normalise(n + 1, 1 - b)
                    for m in range(8):
                        r, t = m // 4, m % 4
                        g = b * TILES + m
                        act.wait_ge(mm_done, done(n * TILES + m + 1))
                        if t == 0:
                            act.wait_ge(stored[r], done(n * 32))
                            act.wait_ge(low_done, done(n * 8))
                        act.activation(high[:, r, t, :], ps[g % 8][:], ACT.Identity,
                                       bias=par[:, t, 2 + r:3 + r]).then_inc(high_done, 1)

            normalise(0, 0)
            with act.Fori(0, CHUNKS // 2 - 1) as i:
                pair(i, False)
            pair(CHUNKS // 2 - 1, True)

        @block.tensor
        def _(pe):
            for s in (mm_done, *stored):
                pe.sem_inc(s, CREDIT)
            pe.wait_ge(par_in, 16 * 3)
            for norm in range(2):
                pe.wait_ge(moments, norm + 1)
                pe.matmul(ps[0][:, 0:KC], gmean[:], mv[:, :, 0], start=True, stop=True).then_inc(gsum, 1)
                pe.wait_ge(spread_ready, norm + 1)
                pe.matmul(ps[1][:, 0:KC], gmean[:], spread[:], start=True, stop=True).then_inc(gsum, 1)
            pe.wait_ge(qn_ready, KC)
            pe.wait_ge(w_in, 16 * 3)
            with pe.Fori(0, CHUNKS // 2) as i:
                for b in range(2):
                    n = i * 2 + b
                    for m in range(TILES):
                        g = b * TILES + m
                        if m == 0 and b == 1:
                            pe.wait_ge(qn_ready, 2 * KC)
                        if m == 0:
                            pe.wait_ge(v_done, done(n * 4))
                        if m == 4:
                            pe.wait_ge(vn_ready, done(n + 1))
                        if m < 4:
                            pe.wait_ge(low_done, done(n * 8))
                        elif m >= 8:
                            pe.wait_ge(low_done, done(n * 8 + m - 8 + 1))
                        r, t = m // 4, m % 4
                        for k in range(KC):
                            if r == 0:
                                lhs, rhs = w["q"][:, k, t * P:(t + 1) * P], xs[:, k, bass.ds(n * BANK, BANK)]
                            elif r == 1:
                                lhs, rhs = w["k"][:, k, t * P:(t + 1) * P], vn[:, b, k, :]
                            else:
                                lhs, rhs = vn[:, b, k, t * P:(t + 1) * P], w["v"][:, k, :]
                            last = pe.matmul(ps[g % 8][:], lhs, rhs, start=(k == 0), stop=(k == KC - 1))
                        last.then_inc(mm_done, 1)


def stage_attention(nc, scr, v_tok, ident_d):
    UNIT = 1024
    UNITS = N // UNIT
    KT = N // P
    PAIRS = KT // 2
    HS = 2 * KT
    OCT = 8
    OCTS = KT // OCT
    ADDS = 5
    SUMS = 3 * HD
    FULL = SUMS + 2
    QT = UNIT // P
    MAXES = QT * CHUNKS
    SLOTS = MAXES + 1
    HEADS_PER_TURN = 2
    TURN = HEADS_PER_TURN * UNITS
    TURNS = HEADS // HEADS_PER_TURN
    ALL = HEADS * UNITS
    PBUF = 2 * OCT
    QBUF = 4
    EARLY = 2
    PER_PAIR = MAXES // PAIRS
    T_AT = PER_PAIR
    with ExitStack() as ctx:
        def sb(name, shape, dt=F32):
            return ctx.enter_context(nc.sbuf_tensor(name, shape, dt))

        def pb(name, shape):
            return ctx.enter_context(nc.psum_tensor(name, shape, F32))

        def sem(name):
            return ctx.enter_context(nc.semaphore(name))

        kst = sb("b_kst", [P, 2, N], F32R)
        qst = sb("b_qst", [P, QBUF, UNIT], F32R)
        vst = sb("b_vst", [P, 2, KT, HD])
        prob = sb("b_prob", [P, PBUF, UNIT])
        sums = sb("b_sums", [P, 2, 2, UNIT])
        ones = sb("b_ones", [P, 1])
        mx = sb("b_mx", [P, QT, CHUNKS])
        mtop = sb("b_mtop", [P, QT])
        mneg = sb("b_mneg", [P, 2 * QT])
        mrow = sb("b_mrow", [2 * QT, P], F32R)
        outn = sb("b_outn", [P, BANK])
        outd = sb("b_outd", [P, BANK])
        ident = sb("b_ident", [P, P])
        pscore = [pb(f"b_pscore{i}", [P, BANK]) for i in range(3)]
        pmax = [pb(f"b_pmax{i}", [P, BANK]) for i in range(3)]
        pout = pb("b_pout", [P, BANK])
        pden = pb("b_pden", [P, BANK])

        consts = sem("b_consts")
        k_in = [sem(f"b_k_in{i}") for i in range(2)]
        q_in = [sem(f"b_q_in{i}") for i in range(QBUF)]
        v_in = sem("b_v_in")
        shift_in = sem("b_shift_in")
        scored = sem("b_scored")
        exped = sem("b_exped")
        times_v_done = sem("b_times_v_done")
        dve_added = sem("b_dve_added")
        pool_added = sem("b_pool_added")
        den_done = sem("b_den_done")
        max_mm = sem("b_max_mm")
        max_read = sem("b_max_read")
        mlink = sem("b_mlink")
        packed = sem("b_packed")
        out_read = sem("b_out_read")
        den_read = sem("b_den_read")
        out_stored = sem("b_out_stored")
        den_stored = sem("b_den_stored")
        counted = (*k_in, *q_in, v_in, shift_in, scored, exped, times_v_done, dve_added, pool_added,
                   den_done, max_mm, max_read, mlink, packed, out_read, den_read, out_stored,
                   den_stored)

        heads = {n: a.rearrange("(h d) n -> h d n", d=HD) for n, a in
                 (("qh", scr.qh), ("ql", scr.ql), ("kh", scr.kh), ("kl", scr.kl))}
        block = ctx.enter_context(nc.Block())

        def score_bank(hs):
            return 1 if hs == HS - 1 else hs % 3

        def max_bank(slot):
            return slot % 3

        def place_of(u, m):
            return m if m < T_AT and not is_unit(u, 0) else m + 1

        def slot_of(u, m):
            return u * SLOTS + place_of(u, m)

        def transposed_slot(u):
            return (u + 1) * SLOTS + (0 if is_unit(u, ALL - 1) else T_AT)

        def is_unit(u, n):
            return isinstance(u, int) and u == n

        def back(bank, n, period):
            return next(d for d in range(1, period) if bank((n - d) % period) == bank(n))

        def units(i):
            for par in range(HEADS_PER_TURN):
                for c in range(UNITS):
                    head = i * HEADS_PER_TURN + par
                    yield head * UNITS + c, head, par, c

        @block.sync
        def _(sp):
            for s in counted:
                sp.sem_inc(s, CREDIT + 1 if s in (max_mm, max_read) else CREDIT)
            sp.dma_start(ident[:], ident_d).then_inc(consts, 16)

            def load_k(head, par):
                for row, name in ((0, "kh"), (HD, "kl"), (2 * HD, "kh")):
                    sp.dma_start(kst[row:row + HD, par, :].bitcast(F32), heads[name][head]).then_inc(k_in[par], 16)

            def load_q(head, c, b):
                for row, name in ((0, "qh"), (HD, "qh"), (2 * HD, "ql")):
                    sp.dma_start(qst[row:row + HD, b, :].bitcast(F32),
                                 heads[name][head, :, c * UNIT:(c + 1) * UNIT]).then_inc(q_in[b], 16)

            def load_shift(u, b):
                sp.wait_ge(max_read, done(transposed_slot(u) + 1))
                for half in range(2):
                    sp.dma_start(qst[SUMS + half:SUMS + half + 1, b, :].bitcast(F32).rearrange(
                        "o (t j) -> o t j", j=P),
                        mrow[half * QT:(half + 1) * QT, :].bitcast(F32)).then_inc(shift_in, 16)

            def store(u, head, c):
                sp.wait_ge(out_read, done(u + 1))
                for half in (1, 0):
                    at = c * UNIT + half * BANK
                    sp.dma_start(scr.att[head, :, :, at:at + BANK],
                                 outn[half * 2 * HD:(half + 1) * 2 * HD, :]).then_inc(out_stored, 16)
                sp.wait_ge(den_read, done(u + 1))
                for half in (1, 0):
                    at = c * UNIT + half * BANK
                    sp.dma_start(scr.att_den[head, :, at:at + BANK],
                                 outd[half * 2 * HD:(half + 1) * 2 * HD:HD, :]).then_inc(den_stored, 16)

            load_k(0, 0)
            load_q(0, 0, 0)
            load_q(0, 1, 1)
            load_k(1, 1)
            load_q(0, 2, 2)
            load_shift(0, 0)

            def turn(i, first, final):
                for u, head, par, c in units(i):
                    place = par * UNITS + c
                    if not (first and place == 0):
                        store(u - 1, head if c else head - 1, (c - 1) % UNITS)
                    sp.wait_ge(scored, done(u * HS))
                    if not (final and place + 3 >= TURN):
                        load_q(i * HEADS_PER_TURN + (place + 3) // UNITS, (place + 3) % UNITS, (place + 3) % QBUF)
                    if c == 0 and not (first and par == 0) and not (final and par == 1):
                        load_k(head + 1, 1 - par)
                    if not (final and place == TURN - 1):
                        load_shift(u + 1, (place + 1) % QBUF)

            turn(0, True, False)
            with sp.Fori(1, TURNS - 1) as i:
                turn(i, False, False)
            turn(TURNS - 1, False, True)
            store(ALL - 1, HEADS - 1, UNITS - 1)
            sp.wait_ge(out_stored, done(ALL * 32))
            sp.wait_ge(den_stored, done(ALL * 32))

        @block.gpsimd
        def _(pool):
            def eight_steps(g, b):
                p = prob[:, b * OCT:(b + 1) * OCT, :]
                a_, b_ = sums[:, b, 0, :], sums[:, b, 1, :]
                pool.wait_ge(den_done, done(g - 1))
                pool.wait_ge(exped, done((g * OCT + 2) * 2))
                pool.tensor_tensor(a_, p[:, 0, :], p[:, 1, :], ALU.add).then_inc(pool_added, 1)
                for n, (acc, step) in enumerate(((a_, 2), (a_, 3), (b_, 6), (b_, 7))):
                    pool.wait_ge(pool_added, done(g * ADDS + n + 1))
                    pool.wait_ge(exped, done((g * OCT + step + 1) * 2))
                    if n == 2:
                        pool.wait_ge(dve_added, done(g + 1))
                    pool.tensor_tensor(acc, acc, p[:, step, :], ALU.add).then_inc(pool_added, 1)

            with pool.Fori(0, ALL * OCTS // 2) as j:
                for b in range(2):
                    eight_steps(j * 2 + b, b)

        def max_part(pair):
            n = (pair + EARLY) % PAIRS * PER_PAIR
            return (1 if pair < PAIRS - EARLY else 2), range(n, n + PER_PAIR)

        @block.tensor
        def _(pe):
            pe.wait_ge(consts, 16 + 4)

            def max_product(u, m, par, b):
                t, j = m // CHUNKS, m % CHUNKS
                pe.wait_ge(max_read, done(slot_of(u, m) - back(max_bank, place_of(u, m), SLOTS) + 1))
                pe.matmul(pmax[max_bank(place_of(u, m))][:], qst[0:SUMS, b, t * P:(t + 1) * P],
                          kst[0:SUMS, par, j * BANK:(j + 1) * BANK], start=True,
                          stop=True).then_inc(max_mm, 1)

            def transpose_shift(u):
                pe.wait_ge(packed, done(u + 1))
                if not is_unit(u, ALL - 1):
                    pe.wait_ge(max_read, done(transposed_slot(u) - back(max_bank, T_AT, SLOTS) + 1))
                pe.transpose(pmax[max_bank(T_AT)][0:2 * QT, 0:P], mneg[:], ident[:]).then_inc(max_mm, 1)

            def scores(u, hs, par, b):
                kt, at = hs // 2, slice(hs % 2 * BANK, (hs % 2 + 1) * BANK)
                pe.wait_ge(exped, done(u * HS + hs - back(score_bank, hs, HS) + 1))
                pe.matmul(pscore[score_bank(hs)][:], kst[0:FULL, par, kt * P:(kt + 1) * P],
                          qst[0:FULL, b, at], start=True, stop=True).then_inc(scored, 1)

            def times_v(u, head, par, c, pair):
                if pair == 0:
                    pe.wait_ge(out_read, done(u))
                    if c == 0:
                        pe.wait_ge(v_in, done(head + 1))
                pe.wait_ge(exped, done(u * HS + (2 * pair + 2) * 2))
                for half in range(2):
                    for odd in range(2):
                        kt = 2 * pair + odd
                        row = (half * 2 + odd) * HD
                        mm = pe.matmul(pout[row:row + HD, :], vst[:, par, kt, :],
                                       prob[:, kt % PBUF, half * BANK:(half + 1) * BANK],
                                       start=(pair == 0), stop=(pair == PAIRS - 1))
                mm.then_inc(times_v_done, 1)

            def denominators(u, o):
                if o == 0:
                    pe.wait_ge(den_read, done(u))
                pe.wait_ge(pool_added, done((u * OCTS + o + 1) * ADDS))
                for half in range(2):
                    for s in range(2):
                        row = (half * 2 + s) * HD
                        mm = pe.matmul(pden[row:row + 1, :], ones[:],
                                       sums[:, o % 2, s, half * BANK:(half + 1) * BANK],
                                       start=(o == 0), stop=(o == OCTS - 1))
                mm.then_inc(den_done, 1)

            pe.wait_ge(q_in[0], done(48))
            pe.wait_ge(k_in[0], done(48))
            for m in range(MAXES):
                max_product(0, m, 0, 0)
            pe.wait_ge(q_in[1], done(48))
            for m in range(EARLY * PER_PAIR):
                if m == T_AT:
                    transpose_shift(0)
                max_product(1, m, 0, 1)

            def turn(i, first, final):
                for u, head, par, c in units(i):
                    place = par * UNITS + c
                    behind = not (first and place == 0)
                    pe.wait_ge(shift_in, done((u + 1) * 32))
                    for pair in range(PAIRS):
                        ahead, products = max_part(pair)
                        target = place + ahead
                        if final and target >= TURN:
                            products = ()
                        t_par, t_buf = target // UNITS % 2, target % QBUF
                        if pair == PAIRS - EARLY and products:
                            pe.wait_ge(q_in[t_buf], done((i * (TURN // QBUF) + target // QBUF + 1) * 48))
                            if target % UNITS == 0:
                                pe.wait_ge(k_in[t_par], done((i + target // TURN + 1) * 48))
                        for part in range(4):
                            scores(u, 4 * pair + part, par, place % QBUF)
                            for m in products[part:part + 1] if part < 3 else ():
                                max_product(u + ahead, m, t_par, t_buf)
                        if pair:
                            times_v(u, head, par, c, pair - 1)
                        elif behind:
                            times_v(u - 1, head, par if c else 1 - par, (c - 1) % UNITS, PAIRS - 1)
                        for m in products[3:]:
                            max_product(u + ahead, m, t_par, t_buf)
                        if pair == PAIRS - EARLY and not (final and place == TURN - 1):
                            transpose_shift(u + 1)
                        if pair % (OCT // 2) == OCT // 2 - 1:
                            o = pair // (OCT // 2)
                            if o:
                                denominators(u, o - 1)
                            elif behind:
                                denominators(u - 1, OCTS - 1)

            turn(0, True, False)
            with pe.Fori(1, TURNS - 1) as i:
                turn(i, False, False)
            turn(TURNS - 1, False, True)
            times_v(ALL - 1, HEADS - 1, 1, UNITS - 1, PAIRS - 1)
            denominators(ALL - 1, OCTS - 1)

        @block.scalar
        def _(act):
            def read_out(u):
                act.wait_ge(times_v_done, done((u + 1) * PAIRS))
                act.wait_ge(out_stored, done(u * 32))
                act.activation(outn[:], pout[:], ACT.Copy).then_inc(out_read, 1)

            def read_den(u):
                act.wait_ge(den_done, done((u + 1) * OCTS))
                act.wait_ge(den_stored, done(u * 32))
                act.activation(outd[:], pden[:], ACT.Copy).then_inc(den_read, 1)

            def unit(u, behind):
                for kt in range(KT):
                    if kt % 2 == 0:
                        act.wait_ge(times_v_done, done(u * PAIRS + kt // 2 - PBUF // 2 + 1))
                    if kt % OCT == 0:
                        act.wait_ge(pool_added, done((u * OCTS + kt // OCT - 1) * ADDS))
                    for half in range(2):
                        hs = 2 * kt + half
                        act.wait_ge(scored, done(u * HS + hs + 1))
                        act.activation(prob[:, kt % PBUF, half * BANK:(half + 1) * BANK],
                                       pscore[score_bank(hs)][:], ACT.Exp,
                                       scale=SCALE).then_inc(exped, 1)
                    if behind and kt == 1:
                        read_out(u - 1)
                    if behind and kt == OCT + 2:
                        read_den(u - 1)

            unit(0, False)
            with act.Fori(1, ALL) as u:
                unit(u, True)
            read_out(ALL - 1)
            read_den(ALL - 1)

        @block.vector
        def _(dve):
            def small(u, n):
                dve.wait_ge(mlink, done(u * 2 + n))

            def read_max(u, m):
                t, j = m // CHUNKS, m % CHUNKS
                dve.wait_ge(max_mm, done(slot_of(u, m) + 1))
                dve.tensor_reduce(mx[:, t, j:j + 1], pmax[max_bank(place_of(u, m))][:], AX.X, ALU.max).then_inc(max_read, 1)

            def pack_shift(u):
                dve.wait_ge(max_read, done(slot_of(u, MAXES - 1) + 1))
                dve.tensor_reduce(mtop[:], mx[:], AX.X, ALU.max).then_inc(mlink, 1)
                small(u, 1)
                dve.wait_ge(max_mm, done(u * SLOTS + T_AT + 1))
                dve.tensor_scalar(mneg[:, 0:QT].bitcast(F32R), mtop[:], -1.0, None, ALU.mult).then_inc(mlink, 1)
                small(u, 2)
                dve.scalar_tensor_tensor(mneg[:, QT:2 * QT], mtop[:], -1.0, mneg[:, 0:QT], ALU.mult,
                                         ALU.subtract).then_inc(packed, 1)

            def copy_shift(u):
                dve.wait_ge(max_mm, done(transposed_slot(u) + 1))
                dve.wait_ge(shift_in, done(u * 32))
                dve.tensor_copy(mrow[:], pmax[max_bank(T_AT)][0:2 * QT, 0:P]).then_inc(max_read, 1)

            def add(g, b):
                dve.wait_ge(den_done, done(g - 1))
                dve.wait_ge(exped, done((g * OCT + 6) * 2))
                dve.tensor_tensor(sums[:, b, 1, :], prob[:, b * OCT + 4, :], prob[:, b * OCT + 5, :],
                                  ALU.add).then_inc(dve_added, 1)

            def copy_v(head, par):
                dve.tensor_copy(vst[:, par, :, :], v_tok[:, :, bass.ds(head * HD, HD)]).then_inc(v_in, 1)

            dve.memset(pden[:], 0.0).then_inc(consts, 1)
            dve.memset(ones[:], 1.0).then_inc(consts, 1)
            for par in range(2):
                dve.memset(kst[SUMS:P, par, :].bitcast(F32), 1.0).then_inc(consts, 1)
            copy_v(0, 0)
            for m in range(MAXES):
                read_max(0, m)
            pack_shift(0)
            for m in range(EARLY * PER_PAIR):
                if m == T_AT:
                    copy_shift(0)
                read_max(1, m)

            def turn(i, final):
                for u, head, par, c in units(i):
                    place = par * UNITS + c
                    for pair in range(PAIRS):
                        ahead, products = max_part(pair)
                        if final and place + ahead >= TURN:
                            products = ()
                        if pair == PAIRS - EARLY and not (final and place == TURN - 1):
                            pack_shift(u + 1)
                        for m in products:
                            read_max(u + ahead, m)
                        if pair == PAIRS - EARLY and not (final and place == TURN - 1):
                            copy_shift(u + 1)
                        if pair % (OCT // 2) == OCT // 2 - 1:
                            o = pair // (OCT // 2)
                            add(u * OCTS + o, o % 2)
                        if c == 1 and pair == 1 and not (final and par == HEADS_PER_TURN - 1):
                            dve.wait_ge(times_v_done, done(head * UNITS * PAIRS))
                            copy_v(head + 1, 1 - par)

            with dve.Fori(0, TURNS - 1) as i:
                turn(i, False)
            turn(TURNS - 1, True)


def stage_output(nc, x, chan_o, woT, scr, x1):
    R2 = 0.5 ** 0.5
    with ExitStack() as ctx:
        def sb(name, shape, dt=F32):
            return ctx.enter_context(nc.sbuf_tensor(name, shape, dt))

        def sem(name):
            return ctx.enter_context(nc.semaphore(name))

        w = sb("c_w", [P, KC, C])
        bo = sb("c_bo", [P, KC])
        bor = sb("c_bor", [P, KC])
        att = sb("c_att", [P, 2, KC, BANK])
        odd = sb("c_odd", [P, 2, KC, BANK])
        rden = sb("c_rden", [P, 2, KC, BANK])
        dens = sb("c_dens", [P, 3, HEADS * N // P])
        ps = [ctx.enter_context(nc.psum_tensor(f"c_ps{i}", [P, BANK], F32)) for i in range(8)]
        w_in = sem("c_w_in")
        x_in = sem("c_x_in")
        att_in = [sem(f"c_att_in{i}") for i in range(2)]
        rden_in = [sem(f"c_rden_in{i}") for i in range(2)]
        den_in = sem("c_den_in")
        den_sum = sem("c_den_sum")
        inverted = sem("c_inverted")
        inv_out = sem("c_inv_out")
        joined = sem("c_joined")
        divided = sem("c_divided")
        scaled = sem("c_scaled")
        mm_done = sem("c_mm_done")
        added = sem("c_added")
        block = ctx.enter_context(nc.Block())

        @block.sync
        def _(sp):
            for s in (*att_in, *rden_in, mm_done, added, joined, divided):
                sp.sem_inc(s, CREDIT)
            for s in range(2):
                sp.dma_start(dens[:, s, :], scr.att_den[:, s, :].rearrange(
                    "h (a n) -> h a n", n=HEADS * N // P)).then_inc(den_in, 16)
            sp.dma_start(w[:], woT.rearrange("(k p) o -> p k o", p=P)).then_inc(w_in, 16)
            sp.dma_start(bo[:], chan_o).then_inc(w_in, 16)
            with sp.Fori(0, CHUNKS // 2) as i:
                for b in range(2):
                    sp.wait_ge(mm_done, done((i * 2 + b) * KC - KC))
                    at = bass.ds((i * 2 + b) * BANK, BANK)
                    if b == 1:
                        sp.wait_ge(x_in, 16 * (i + 1))
                    for k in range(KC):
                        hs = slice(k * P // HD, (k + 1) * P // HD)
                        sp.dma_start(att[:, b, k, :], scr.att[hs, 0, :, at]).then_inc(att_in[b], 16)
                        sp.dma_start(odd[:, b, k, :], scr.att[hs, 1, :, at]).then_inc(att_in[b], 16)
                    if b == 0:
                        both = bass.ds(i * 2 * BANK, 2 * BANK)
                        sp.dma_start(x1[:, :, both], x.rearrange("(k p) n -> p k n", p=P)[:, :, both]).then_inc(x_in, 16)

        @block.tensor
        def _(pe):
            pe.wait_ge(w_in, 32)
            with pe.Fori(0, CHUNKS // 2) as i:
                for b in range(2):
                    n = i * 2 + b
                    pe.wait_ge(divided, done(n + 1))
                    for t in range(KC):
                        pe.wait_ge(added, done(n * KC + t + 1 - 8))
                        for k in range(KC):
                            mm = pe.matmul(ps[b * KC + t][:], w[:, k, t * P:(t + 1) * P], att[:, b, k, :],
                                           start=(k == 0), stop=(k == KC - 1))
                        mm.then_inc(mm_done, 1)

        @block.scalar
        def _(act):
            act.wait_ge(w_in, 32)
            act.mul(bor[:], bo[:], R2).then_inc(scaled, 1)
            act.wait_ge(inverted, 1)
            act.dma_start(scr.att_rden.rearrange("h (a n) -> h a n", n=HEADS * N // P),
                          dens[:, 2, :]).then_inc(inv_out, 16)
            act.wait_ge(scaled, 1)
            act.wait_ge(inv_out, 16)
            with act.Fori(0, CHUNKS // 2) as i:
                for b in range(2):
                    n = i * 2 + b
                    act.wait_ge(divided, done(n - 1))
                    for k in range(KC):
                        hs = slice(k * P // HD, (k + 1) * P // HD)
                        act.dma_start(rden[:, b, k, :], scr.att_rden[hs, bass.ds(n * BANK, BANK)].unsqueeze(1)
                                      .to_broadcast([P // HD, HD, BANK])).then_inc(rden_in[b], 16)
                act.wait_ge(x_in, 16 * (i + 1))
                for k in range(KC):
                    at = x1[:, k, bass.ds(i * 2 * BANK, 2 * BANK)]
                    act.activation(at, at, ACT.Identity, bias=bor[:, k:k + 1], scale=R2).then_inc(scaled, 1)

        @block.vector
        def _(dve):
            dve.wait_ge(den_in, 32)
            dve.tensor_tensor(dens[:, 0, :], dens[:, 0, :], dens[:, 1, :], ALU.add).then_inc(den_sum, 1)
            dve.wait_ge(den_sum, 1)
            dve.reciprocal(dens[:, 2, :], dens[:, 0, :]).then_inc(inverted, 1)

            def divide(n, turn, b):
                dve.wait_ge(att_in[b], done((turn + 1) * 16 * 2 * KC))
                dve.tensor_tensor(att[:, b, :, :], att[:, b, :, :], odd[:, b, :, :], ALU.add).then_inc(joined, 1)
                dve.wait_ge(joined, done(n + 1))
                dve.wait_ge(rden_in[b], done((turn + 1) * 16 * KC))
                dve.tensor_tensor(att[:, b, :, :], att[:, b, :, :], rden[:, b, :, :],
                                  ALU.mult).then_inc(divided, 1)

            divide(0, 0, 0)

            def pair(i, final):
                for b in range(2):
                    n = i * 2 + b
                    if not (final and b == 1):
                        divide(n + 1, i + b, 1 - b)
                    if b == 0:
                        dve.wait_ge(scaled, (i + 1) * KC + 1)
                    for t in range(KC):
                        dve.wait_ge(mm_done, done(n * KC + t + 1))
                        at = x1[:, t, bass.ds(n * BANK, BANK)]
                        dve.scalar_tensor_tensor(at, ps[b * KC + t][:], R2, at, ALU.mult,
                                                 ALU.add).then_inc(added, 1)

            with dve.Fori(0, CHUNKS // 2 - 1) as i:
                pair(i, False)
            pair(CHUNKS // 2 - 1, True)


GH = 8
ROLES = 3
GROUPS = C // P
TAPS = 5
PAD = IMG + TAPS - 1
ROWS = BANK // IMG
HPG = P // GH
EPS_ATT = 1e-15


def stage_linear(nc, w_all, dw_all, pw_all, mask_d, heads_d, ident_d, scr, x1):
    DVE_CHUNKS = 6
    UNROLL = 2 * ROLES
    TURNS = GROUPS * ROLES // UNROLL
    RING = 3
    OUT_RING = 2
    EDGE = DVE_CHUNKS * ROWS
    K, V, Q = range(ROLES)
    TK_CHUNKS = CHUNKS + CHUNKS - DVE_CHUNKS

    def tk_at(part, n):
        first = 4 * (n if part == 0 or n < DVE_CHUNKS else CHUNKS + n - DVE_CHUNKS)
        return slice(first, first + 4)

    def order():
        out = []
        late = lambda t: [(t, 1, n) for n in range(DVE_CHUNKS)]
        for t in range(UNROLL):
            out += [(t, 0, n) for n in range(CHUNKS)]
            if t:
                out += late(t - 1)
            out += [(t, 1, n) for n in range(DVE_CHUNKS, CHUNKS)]
        return out + late(UNROLL - 1)

    PIECES = order()
    NP = len(PIECES)
    at = {piece: p for p, piece in enumerate(PIECES)}
    WAITING = [p for p in range(NP) if PIECES[p][1:] == (1, 0)]
    V_PIECES = [p for p in range(NP) if PIECES[p][0] % ROLES == V]
    last_piece = {(t, part): max(p for p, (a, b, _) in enumerate(PIECES) if (a, b) == (t, part))
                  for t in range(UNROLL) for part in range(2)}
    first_piece = {(t, part): min(p for p, (a, b, _) in enumerate(PIECES) if (a, b) == (t, part))
                   for t in range(UNROLL) for part in range(2)}

    with ExitStack() as ctx:
        def sb(name, shape, dt=F32):
            return ctx.enter_context(nc.sbuf_tensor(name, shape, dt))

        def pb(name):
            return ctx.enter_context(nc.psum_tensor(name, [P, BANK], F32))

        def sem(name):
            return ctx.enter_context(nc.semaphore(name))

        w = sb("d_w", [P, 2, KC, P])
        dw = sb("d_dw", [P, 2, TAPS * TAPS])
        pw = sb("d_pw", [P, 2, P])
        bd = sb("d_bd", [P, 2, P])
        with nc.sbuf_tensor("d_wtap", [P, TAPS * TAPS, P], F32) as wtap:
            pass
        wlow = sb("d_wlow", [P, TAPS * TAPS, P], F32R)
        whigh = sb("d_whigh", [P, TAPS * TAPS, P], F32R)
        yhigh = sb("d_yhigh", [P, PAD - EDGE, PAD], F32R)
        ylow = sb("d_ylow", [P, PAD - EDGE, PAD], F32R)
        ypad = sb("d_ypad", [P, 2, PAD, PAD])
        dsum = sb("d_dsum", [P, 2, DVE_CHUNKS * BANK])
        piece = sb("d_piece", [P, RING, BANK])
        tk = sb("d_tk", [P, 4 * TK_CHUNKS, P])
        tv = sb("d_tv", [P, 2, 4, P + 1])
        vks = sb("d_vks", [P, P + 1])
        num_w = sb("d_num_w", [P, 2, P])
        den_w = sb("d_den_w", [P, 2, HPG])
        num = sb("d_num", [P, OUT_RING, BANK])
        den = sb("d_den", [HPG, OUT_RING, BANK])
        mask = sb("d_mask", [P, P])
        hmask = sb("d_hmask", [P, HPG])
        ident = sb("d_ident", [P, P])
        pmain = [pb(f"d_pmain{i}") for i in range(RING)]
        ptr = [pb(f"d_ptr{i}") for i in range(2)]
        pnum, pden, pvk = pb("d_pnum"), pb("d_pden"), pb("d_pvk")

        consts = sem("d_consts")
        zeroed = sem("d_zeroed")
        loaded = [sem(f"d_loaded{i}") for i in range(2)]
        built = sem("d_built")
        bd_made = sem("d_bd_made")
        w_high = sem("d_w_high")
        y_high = sem("d_y_high")
        split = sem("d_split")
        main_done = sem("d_main_done")
        main_read = sem("d_main_read")
        post_done = sem("d_post_done")
        post_read = sem("d_post_read")
        vk_done = sem("d_vk_done")
        vk_read = sem("d_vk_read")
        vk_used = sem("d_vk_used")
        dlink = sem("d_dlink")
        stored = [sem(f"d_stored{i}") for i in range(OUT_RING)]
        TAPN = TAPS * TAPS

        block = ctx.enter_context(nc.Block())

        @block.sync
        def _(sp):
            for s in (*loaded, built, bd_made, w_high, y_high, split, main_done, main_read, post_done, post_read, vk_done,
                      vk_read, vk_used, dlink, *stored):
                sp.sem_inc(s, CREDIT)
            for dst, src in ((mask, mask_d), (hmask, heads_d), (ident, ident_d)):
                sp.dma_start(dst[:], src).then_inc(consts, 16)

            def load(i, t):
                tile, b = i * UNROLL + t, t % 2
                sp.wait_ge(dlink, done((i * UNROLL + t - 1) * TAPN))
                sp.wait_ge(built, done(i * UNROLL + t - 1))
                sp.dma_start(w[:, b, :, :], w_all[tile].rearrange("(k p) o -> p k o", p=P)).then_inc(loaded[b], 16)
                sp.dma_start(dw[:, b, :], dw_all[tile]).then_inc(loaded[b], 16)
                sp.dma_start(pw[:, b, :], pw_all[tile]).then_inc(loaded[b], 16)

            for dst, src in ((w[:, 0, :, :], w_all[0].rearrange("(k p) o -> p k o", p=P)),
                             (dw[:, 0, :], dw_all[0]), (pw[:, 0, :], pw_all[0])):
                sp.dma_start(dst, src).then_inc(loaded[0], 16)

            def turn(i, final):
                for p, (t, part, n) in enumerate(PIECES):
                    if t % ROLES == Q:
                        group = i * 2 + t // ROLES
                        sp.wait_ge(post_read, done(i * NP + p + 1))
                        sp.dma_start(scr.num[part, group, :, n * BANK:(n + 1) * BANK],
                                     num[:, p % OUT_RING, :]).then_inc(stored[p % OUT_RING], 16)
                        sp.dma_start(scr.den[part, group, :, n * BANK:(n + 1) * BANK],
                                     den[:, p % OUT_RING, :]).then_inc(stored[p % OUT_RING], 16)
                    if part == 0 and n == CHUNKS - 1 and not (final and t == UNROLL - 1):
                        load(i, t + 1)

            with sp.Fori(0, TURNS - 1) as i:
                turn(i, False)
            turn(TURNS - 1, True)
            for r in range(OUT_RING):
                mine = sum(t % ROLES == Q and p % OUT_RING == r for p, (t, _, _) in enumerate(PIECES))
                sp.wait_ge(stored[r], done(TURNS * mine * 32))

        @block.gpsimd
        def _(pool):
            pool.wait_ge(consts, 48)

            def build(i, t):
                b = t % 2
                pool.wait_ge(loaded[b], done((i * (UNROLL // 2) + t // 2 + 1) * 48))
                if t >= 2:
                    pool.wait_ge(main_done, done(i * NP + last_piece[t - 2, 1] + 1))
                else:
                    pool.wait_ge(main_done, done(i * NP))
                tile = i * UNROLL + t
                pool.tensor_tensor(bd[:, b, :], pw[:, b, :], mask[:], ALU.mult).then_inc(bd_made, 1)
                pool.wait_ge(bd_made, done(tile + 1))
                pool.wait_ge(main_done, done(i * NP + (at[t - 1, 1, CHUNKS - 1] + 1 if t else 0)))
                pool.tensor_tensor(wtap[:, 0, :], bd[:, b, :], dw[:, b, 0:1].to_broadcast([P, P]), ALU.mult)
                for tap in range(1, TAPN):
                    last = pool.tensor_scalar(wtap[:, tap, :], bd[:, b, :], dw[:, b, tap:tap + 1],
                                              None, ALU.mult)
                last.then_inc(built, 1)

            def lows(i, t):
                tile = i * UNROLL + t
                pool.wait_ge(w_high, done(tile + 1))
                pool.tensor_tensor(wlow[:], wtap[:], whigh[:].bitcast(F32), ALU.subtract)
                pool.wait_ge(y_high, done(tile + 1))
                pool.tensor_tensor(ylow[:], ypad[:, t % 2, EDGE:, :], yhigh[:].bitcast(F32),
                                   ALU.subtract).then_inc(split, 1)

            def blocks(i, g, part):
                count = (i * 2 + g) * 2 + part
                pool.wait_ge(vk_read, done(count + 1))
                t = g * ROLES + Q
                if g:
                    pool.wait_ge(post_done, done(i * NP + last_piece[t - ROLES, part] + 1))
                else:
                    pool.wait_ge(post_done, done(i * NP))
                pool.tensor_tensor(num_w[:, part, :], vks[:, 0:P], mask[:], ALU.mult)
                pool.tensor_scalar(den_w[:, part, :], hmask[:], vks[:, P:P + 1], None,
                                   ALU.mult).then_inc(vk_used, 1)

            with pool.Fori(0, TURNS) as i:
                for g in range(2):
                    build(i, g * ROLES + K)
                    lows(i, g * ROLES + K)
                    build(i, g * ROLES + V)
                    lows(i, g * ROLES + V)
                    blocks(i, g, 0)
                    build(i, g * ROLES + Q)
                    lows(i, g * ROLES + Q)
                    blocks(i, g, 1)

        @block.tensor
        def _(pe):
            pe.wait_ge(consts, 48)
            pe.wait_ge(zeroed, 4)

            def main(i, p):
                t, part, n = PIECES[p]
                b = t % 2
                tile = i * UNROLL + t
                pe.wait_ge(main_read, done(i * NP + p + 1 - RING))
                out = pmain[p % RING][:]
                if part == 0:
                    if n == 0:
                        pe.wait_ge(loaded[b], done((i * (UNROLL // 2) + t // 2 + 1) * 48))
                    for k in range(KC):
                        mm = pe.matmul(out, w[:, b, k, :], x1[:, k, n * BANK:(n + 1) * BANK],
                                       start=(k == 0), stop=(k == KC - 1))
                elif n >= DVE_CHUNKS:
                    if n == DVE_CHUNKS:
                        pe.wait_ge(split, done(tile + 1))
                    products = [(tap, *pair) for tap in range(TAPN)
                                for pair in ((whigh, yhigh), (wlow, yhigh), (whigh, ylow))]
                    for k, (tap, weights, image) in enumerate(products):
                        row, dx = n * ROWS - EDGE + tap // TAPS, tap % TAPS
                        mm = pe.matmul(out.rearrange("p (r c) -> p r c", c=IMG), weights[:, tap, :],
                                       image[:, row:row + ROWS, dx:dx + IMG],
                                       start=(k == 0), stop=(k == len(products) - 1))
                else:
                    if n == 0:
                        pe.wait_ge(dlink, done((tile + 1) * TAPN))
                        pe.wait_ge(built, done(tile + 1))
                    mm = pe.matmul(out, bd[:, b, :], dsum[:, b, n * BANK:(n + 1) * BANK],
                                   start=True, stop=True)
                mm.then_inc(main_done, 1)

            def post(i, p):
                t, part, n = PIECES[p]
                role, group = t % ROLES, i * 2 + t // ROLES
                pe.wait_ge(main_read, done(i * NP + p + 1))
                if role == Q:
                    if p == first_piece[t, part]:
                        pe.wait_ge(vk_used, done(group * 2 + part + 1))
                    pe.wait_ge(post_read, done(i * NP + p))
                    pe.matmul(pnum[:], num_w[:, part, :], piece[:, p % RING, :], start=True, stop=True)
                    pe.matmul(pden[0:HPG, :], den_w[:, part, :], piece[:, p % RING, :], start=True,
                              stop=True).then_inc(post_done, 1)
                else:
                    pe.wait_ge(post_read, done(i * NP + p - 1))
                    for s in range(4):
                        tr = pe.transpose(ptr[p % 2][:, s * P:(s + 1) * P],
                                          piece[:, p % RING, s * P:(s + 1) * P], ident[:])
                    tr.then_inc(post_done, 1)

            def times_k(i, p):
                t, part, n = PIECES[p]
                if t % ROLES != V:
                    return
                pe.wait_ge(post_read, done(i * NP + p + 1))
                first, last = p == first_piece[t, part], p == last_piece[t, part]
                if first:
                    pe.wait_ge(vk_read, done((i * 2 + t // ROLES) * 2 + part))
                for s in range(4):
                    mm = pe.matmul(pvk[:, 0:P + 1], tk[:, tk_at(part, n).start + s, :], tv[:, V_PIECES.index(p) % 2, s, :],
                                   start=(first and s == 0), stop=(last and s == 3))
                mm.then_inc(vk_done, 1)

            with pe.Fori(0, TURNS) as i:
                for p in range(NP + 2):
                    if p in WAITING:
                        times_k(i, p - 2)
                    if p < NP:
                        main(i, p)
                    if p >= 2 and p not in WAITING:
                        times_k(i, p - 2)
                    if 1 <= p <= NP:
                        post(i, p - 1)

        @block.scalar
        def _(act):
            act.wait_ge(zeroed, 4)

            def read_main(i, p):
                t, part, n = PIECES[p]
                b, role = t % 2, t % ROLES
                tile = i * UNROLL + t
                act.wait_ge(main_done, done(i * NP + p + 1))
                src = pmain[p % RING][:]
                if part == 0:
                    if n == 0:
                        if t:
                            act.wait_ge(dlink, done((tile - 1) * TAPN))
                        act.wait_ge(post_done, done(i * NP + (at[t - 2, 1, CHUNKS - 1] + 1 if t >= 2 else 0)))
                    act.activation(ypad[:, b, 2 + n * ROWS:2 + (n + 1) * ROWS, 2:2 + IMG],
                                   src.rearrange("p (r c) -> p r c", c=IMG), ACT.Copy)
                act.wait_ge(post_done, done(i * NP + p + 1 - RING))
                act.activation(piece[:, p % RING, :], src,
                               ACT.Copy if role == V else ACT.Relu).then_inc(main_read, 1)
                if part == 0 and n == 6:
                    act.wait_ge(built, done(tile + 1))
                    act.activation(whigh[:], wtap[:], ACT.Copy).then_inc(w_high, 1)
                if part == 0 and n == CHUNKS - 1:
                    act.wait_ge(main_read, done(i * NP + p + 1))
                    act.activation(yhigh[:], ypad[:, b, EDGE:, :], ACT.Copy).then_inc(y_high, 1)

            def read_post(i, p):
                t, part, n = PIECES[p]
                role, group = t % ROLES, i * 2 + t // ROLES
                act.wait_ge(post_done, done(i * NP + p + 1))
                if role == K:
                    if p == first_piece[t, part]:
                        act.wait_ge(vk_read, done(group * 2))
                    if part == 1 and n < DVE_CHUNKS:
                        act.wait_ge(vk_done, done(i * len(V_PIECES) + V_PIECES.index(at[t + 1, 0, n]) + 1))
                    act.activation(tk[:, tk_at(part, n), :],
                                   ptr[p % 2][:].rearrange("p (s c) -> p s c", c=P),
                                   ACT.Copy).then_inc(post_read, 1)
                elif role == V:
                    k = V_PIECES.index(p)
                    act.wait_ge(vk_done, done(i * len(V_PIECES) + k - 1))
                    act.activation(tv[:, k % 2, :, 0:P], ptr[p % 2][:].rearrange("p (s c) -> p s c", c=P),
                                   ACT.Copy).then_inc(post_read, 1)
                else:
                    r = p % OUT_RING
                    mine = [x for x in range(NP) if PIECES[x][0] % ROLES == Q and x % OUT_RING == r]
                    act.wait_ge(stored[r], done((i * len(mine) + mine.index(p)) * 32))
                    act.activation(num[:, r, :], pnum[:], ACT.Copy)
                    act.activation(den[:, r, :], pden[0:HPG, :], ACT.Copy, bias=EPS_ATT).then_inc(post_read, 1)

            def read_vk(i, p):
                t, part, _ = PIECES[p]
                if t % ROLES == V and p == last_piece[t, part]:
                    count = (i * 2 + t // ROLES) * 2 + part
                    act.wait_ge(vk_done, done(i * len(V_PIECES) + V_PIECES.index(p) + 1))
                    act.wait_ge(vk_used, done(count))
                    act.activation(vks[:], pvk[:, 0:P + 1], ACT.Copy).then_inc(vk_read, 1)

            with act.Fori(0, TURNS) as i:
                for p in range(NP + 2):
                    if p in WAITING:
                        read_vk(i, p - 2)
                    if p < NP:
                        read_main(i, p)
                    if p >= 2 and p not in WAITING:
                        read_vk(i, p - 2)
                    if 1 <= p <= NP:
                        read_post(i, p - 1)

        @block.vector
        def _(dve):
            for b in range(2):
                dve.memset(ypad[:, b, :, :], 0.0).then_inc(zeroed, 1)
                dve.memset(tv[:, b, :, P:P + 1], 1.0).then_inc(zeroed, 1)
            with dve.Fori(0, TURNS) as i:
                for t in range(UNROLL):
                    b = t % 2
                    tile = i * UNROLL + t
                    dve.wait_ge(loaded[b], done((i * (UNROLL // 2) + t // 2 + 1) * 48))
                    dve.wait_ge(main_read, done(i * NP + last_piece[t, 0] + 1))
                    dve.wait_ge(main_done, done(i * NP + (at[t - 2, 1, DVE_CHUNKS - 1] + 1 if t >= 2 else 0)))
                    acc = dsum[:, b, :].rearrange("p (r c) -> p r c", c=IMG)
                    for tap in range(TAPN):
                        dy, dx = tap // TAPS, tap % TAPS
                        src = ypad[:, b, dy:dy + DVE_CHUNKS * ROWS, dx:dx + IMG]
                        if tap == 0:
                            add = dve.tensor_scalar(acc, src, dw[:, b, tap:tap + 1], None, ALU.mult)
                        else:
                            dve.wait_ge(dlink, done(tile * TAPN + tap))
                            add = dve.scalar_tensor_tensor(acc, src, dw[:, b, tap:tap + 1], acc,
                                                           ALU.mult, ALU.add)
                        add.then_inc(dlink, 1)


def stage_project(nc, wprojT, chan_bn, scr, x1, out):
    BN_EPS = 1e-5
    MS = 2 * GROUPS
    HALF = N // 2
    with ExitStack() as ctx:
        def sb(name, shape, dt=F32):
            return ctx.enter_context(nc.sbuf_tensor(name, shape, dt))

        def sem(name):
            return ctx.enter_context(nc.semaphore(name))

        w = sb("f_w", [P, MS, C])
        par = sb("f_par", [P, KC, 2])
        num = sb("f_num", [P, 2, MS, BANK])
        rden = sb("f_rden", [P, 2, GROUPS, BANK])
        proj = sb("f_proj", [P, KC, N])
        dens = proj[:, 0:2, :]
        stats = sb("f_stats", [P, KC, CHUNKS, 6])
        mv = sb("f_mv", [P, KC, 2])
        coef = sb("f_coef", [P, 2, KC])
        var = sb("f_var", [P, KC])
        sd = sb("f_sd", [P, KC])
        rstd = sb("f_rstd", [P, KC])
        tmp = sb("f_tmp", [P, KC])
        ps = [ctx.enter_context(nc.psum_tensor(f"f_ps{i}", [P, BANK], F32)) for i in range(8)]

        den_in = [sem(f"f_den_in{i}") for i in range(2)]
        inverted = sem("f_inverted")
        inv_out = [sem(f"f_inv_out{i}") for i in range(2)]
        w_in = sem("f_w_in")
        num_in = [sem(f"f_num_in{i}") for i in range(2)]
        rden_in = [sem(f"f_rden_in{i}") for i in range(2)]
        divided = sem("f_divided")
        mm_done = sem("f_mm_done")
        copied = sem("f_copied")
        measured = sem("f_measured")
        link_s = sem("f_link")
        var_ready = sem("f_var_ready")
        root = sem("f_root")
        coef_ready = sem("f_coef_ready")
        scaled = sem("f_scaled")
        summed = sem("f_summed")
        stored = sem("f_stored")
        block = ctx.enter_context(nc.Block())

        @block.sync
        def _(sp):
            for s in (*num_in, *rden_in, divided, mm_done, copied, measured):
                sp.sem_inc(s, CREDIT)

            def store_inverse(n, b):
                at = bass.ds(n * BANK, BANK)
                sp.wait_ge(inverted, n + 1)
                sp.dma_start(scr.rden[:, at], dens[:, 1, at]).then_inc(inv_out[b], 16)

            for s, at in zip(den_in, (slice(0, BANK), slice(BANK, N))):
                sp.dma_start(dens[:, 0, at], scr.den.rearrange("a g h n -> (a g h) n")[:, at]).then_inc(s, 16)
            sp.dma_start(w[:], wprojT.rearrange("(m p) o -> p m o", p=P)).then_inc(w_in, 16)
            sp.dma_start(par[:], chan_bn).then_inc(w_in, 16)
            def turn(i, final):
                for b in range(2):
                    n = i * 2 + b
                    at = bass.ds(n * BANK, BANK)
                    sp.wait_ge(mm_done, done(n * KC - KC))
                    sp.dma_start(num[:, b, :, :], scr.num.rearrange("a g p n -> p (a g) n")[
                        :, :, at]).then_inc(num_in[b], 16)
                    sp.wait_ge(inv_out[b], 16 * (i + 1))
                    for part in range(2):
                        sp.wait_ge(divided, done(n * 2 + part - 1))
                        for g in range(GROUPS):
                            row = (part * GROUPS + g) * HPG
                            sp.dma_start(rden[:, part, g, :], scr.rden[row:row + HPG, at].unsqueeze(1)
                                         .to_broadcast([HPG, GH, BANK])).then_inc(rden_in[part], 16)
                    if not final:
                        store_inverse(n + 2, b)

            store_inverse(0, 0)
            store_inverse(1, 1)
            with sp.Fori(0, CHUNKS // 2 - 1) as i:
                turn(i, False)
            turn(CHUNKS // 2 - 1, True)
            for t in range(KC):
                for h in range(2):
                    sp.wait_ge(summed, t * 2 + h + 1)
                    sp.dma_start(out[t * P:(t + 1) * P, h * HALF:(h + 1) * HALF],
                                 proj[:, t, h * HALF:(h + 1) * HALF]).then_inc(stored, 16)
            sp.wait_ge(stored, KC * 2 * 16)

        @block.tensor
        def _(pe):
            pe.wait_ge(w_in, 32)
            with pe.Fori(0, CHUNKS // 2) as i:
                for b in range(2):
                    n = i * 2 + b
                    for t in range(KC):
                        if t == 0:
                            pe.wait_ge(divided, done(n * 2 + 2))
                        pe.wait_ge(copied, done(n * KC + t + 1 - 8))
                        for m in range(MS):
                            mm = pe.matmul(ps[b * KC + t][:], w[:, m, t * P:(t + 1) * P], num[:, b, m, :],
                                           start=(m == 0), stop=(m == MS - 1))
                        mm.then_inc(mm_done, 1)

        @block.scalar
        def _(act):
            with act.Fori(0, CHUNKS // 2) as i:
                for b in range(2):
                    n = i * 2 + b
                    for t in range(KC):
                        act.wait_ge(mm_done, done(n * KC + t + 1))
                        act.activation(proj[:, t, bass.ds(n * BANK, BANK)], ps[b * KC + t][:],
                                       ACT.Copy).then_inc(copied, 1)
            act.wait_ge(var_ready, 1)
            act.activation(sd[:], var[:], ACT.Sqrt).then_inc(root, 1)
            act.wait_ge(coef_ready, 1)
            for t in range(KC):
                for h in range(2):
                    at = proj[:, t, h * HALF:(h + 1) * HALF]
                    act.activation(at, at, ACT.Identity, bias=coef[:, 1, t:t + 1],
                                   scale=coef[:, 0, t:t + 1]).then_inc(scaled, 1)

        @block.vector
        def _(dve):
            links = 0

            def link(ins):
                nonlocal links
                links += 1
                ins.then_inc(link_s, 1)
                dve.wait_ge(link_s, links)

            def invert(n):
                at = slice(n * BANK, (n + 1) * BANK)
                if n < 2:
                    dve.wait_ge(den_in[n], 16)
                dve.reciprocal(dens[:, 1, at], dens[:, 0, at]).then_inc(inverted, 1)

            def divide(n, b):
                for part in range(2):
                    if part == 0:
                        dve.wait_ge(num_in[b], done(16 * (n // 2 + 1)))
                    dve.wait_ge(rden_in[part], done(64 * (n + 1)))
                    at = num[:, b, part * GROUPS:(part + 1) * GROUPS, :]
                    dve.tensor_tensor(at, at, rden[:, part, :, :], ALU.mult).then_inc(divided, 1)

            def measure(n):
                for t in range(KC):
                    dve.wait_ge(copied, done(n * KC + t + 1))
                    dve.bn_stats(stats[:, t, n, :], proj[:, t, n * BANK:(n + 1) * BANK]).then_inc(measured, 1)

            invert(0)
            invert(1)
            divide(0, 0)
            for n in range(CHUNKS):
                if n + 2 < CHUNKS:
                    invert(n + 2)
                if n + 1 < CHUNKS:
                    divide(n + 1, (n + 1) % 2)
                measure(n)
            dve.wait_ge(w_in, 32)
            dve.wait_ge(measured, done(KC * CHUNKS))
            for t in range(KC):
                last = dve.bn_aggr(mv[:, t, :], stats[:, t, :, :].rearrange("p j s -> p (j s)"))
            link(last)
            dve.tensor_scalar(var[:], mv[:, :, 1], BN_EPS, None, ALU.add).then_inc(var_ready, 1)
            dve.wait_ge(root, 1)
            link(dve.reciprocal(rstd[:], sd[:]))
            link(dve.tensor_tensor(tmp[:], rstd[:], rstd[:], ALU.mult))
            link(dve.tensor_tensor(tmp[:], tmp[:], var[:], ALU.mult))
            link(dve.tensor_scalar(tmp[:], tmp[:], -0.5, 1.5, ALU.mult, ALU.add))
            link(dve.tensor_tensor(rstd[:], rstd[:], tmp[:], ALU.mult))
            link(dve.tensor_tensor(coef[:, 0, :], rstd[:], par[:, :, 0], ALU.mult))
            link(dve.tensor_tensor(tmp[:], mv[:, :, 0], coef[:, 0, :], ALU.mult))
            dve.tensor_tensor(coef[:, 1, :], par[:, :, 1], tmp[:], ALU.subtract).then_inc(coef_ready, 1)
            for t in range(KC):
                for h in range(2):
                    dve.wait_ge(scaled, t * 2 + h + 1)
                    at = slice(h * HALF, (h + 1) * HALF)
                    dve.tensor_tensor(proj[:, t, at], proj[:, t, at], x1[:, t, at], ALU.add).then_inc(summed, 1)


def conv_seq(nc, x, chan, wqT, wkT, wvT, bv, bo, woT, w_all, dw_all, pw_all, wprojT, chan_bn,
             group_mean, mask, hmask, ident, out):
    scr = Scratch(nc)
    with nc.sbuf_tensor("v_tok", [P, N // P, C], F32) as v_tok:
        stage_qkv(nc, x, chan, wqT, wkT, wvT, bv, group_mean, scr, v_tok)
        stage_attention(nc, scr, v_tok, ident)
    with nc.sbuf_tensor("x1", [P, KC, N], F32) as x1:
        stage_output(nc, x, bo, woT, scr, x1)
        stage_linear(nc, w_all, dw_all, pw_all, mask, hmask, ident, scr, x1)
        stage_project(nc, wprojT, chan_bn, scr, x1, out)


def kernel(**inputs):
    import numpy as np
    import concourse.bacc as bacc
    from concourse.bass_utils import run_bass_kernel_spmd as run

    def by_channel(*vectors):
        return np.stack([np.asarray(v).reshape(KC, P) for v in vectors], -1).transpose(1, 0, 2)

    a = {n: np.asarray(v) for n, v in inputs.items()}
    l0 = {n[len("L0_conv_"):]: v for n, v in a.items() if n.startswith("L0_conv_")}
    l1 = {n[len("L1_conv_"):]: v for n, v in a.items() if n.startswith("L1_conv_")}
    roles = [1, 2, 0]
    w_all = l1["w_qkv"].reshape(GROUPS, HPG, ROLES, GH, C)[:, :, roles].transpose(0, 2, 4, 1, 3)
    dw_all = l1["w_dw"].reshape(GROUPS, HPG, ROLES, GH, TAPS * TAPS)[:, :, roles].transpose(0, 2, 1, 3, 4)
    pw = l1["w_pw"].reshape(GROUPS, HPG, ROLES, GH, GH)[:, :, roles].transpose(0, 2, 1, 4, 3)
    pw_all = np.tile(pw.reshape(GROUPS * ROLES, P, GH), (1, 1, HPG))
    eye = np.eye(P, dtype=np.float32)
    arrays = {
        "x": a["x"].reshape(C, N),
        "chan": by_channel(l0["gn_w"], l0["gn_b"], l0["bq"], l0["bk"]),
        "wqT": l0["wq"].T, "wkT": l0["wk"].T, "wvT": l0["wv"].T, "bv": l0["bv"],
        "bo": by_channel(l0["bo"])[:, :, 0],
        "woT": l0["wo"].T,
        "w_all": w_all.reshape(GROUPS * ROLES, C, P),
        "dw_all": dw_all.reshape(GROUPS * ROLES, P, TAPS * TAPS),
        "pw_all": pw_all,
        "wprojT": l1["w_proj"].T,
        "chan_bn": by_channel(l1["bn_gamma"], l1["bn_beta"]),
        "group_mean": np.kron(np.eye(P // GN_GROUP), np.full((GN_GROUP, GN_GROUP), 1.0 / GN_GROUP)).astype(np.float32),
        "mask": np.kron(np.eye(HPG), np.ones((GH, GH))).astype(np.float32),
        "hmask": np.kron(np.eye(HPG), np.ones((GH, 1))).astype(np.float32),
        "ident": eye,
    }
    nc = bacc.Bacc("TRN2", target_bir_lowering=False, num_devices=1)
    args, ins = [], {}
    for name, v in arrays.items():
        v = np.ascontiguousarray(v)
        ins[f"in_{name}"] = v
        args.append(nc.dram_tensor(f"in_{name}", v.shape, mybir.dt.from_np(v.dtype), kind="ExternalInput").ap())
    out = nc.dram_tensor("out_0", (1, C, IMG, IMG), F32, kind="ExternalOutput").ap()
    conv_seq(nc, *args, out.rearrange("b c h w -> (b c) (h w)"))
    r = run(nc, [ins], core_ids=[0])
    return r.results[0]["out_0"]
```
